# Optimizing a Trainium2 kernel written in Bass

```python
import numpy as np
import jax
import jax.numpy as jnp

def _softmax(x, axis=-1):
    return jax.nn.softmax(x, axis=axis)

def _gelu(x):
    return jax.nn.gelu(x, approximate=True)

def _silu(x):
    return jax.nn.silu(x)

def _sigmoid(x):
    return jax.nn.sigmoid(x)

def _layernorm(x, axis=-1, eps=1e-05):
    m = jnp.mean(x, axis=axis, keepdims=True)
    v = jnp.var(x, axis=axis, keepdims=True)
    return (x - m) / jnp.sqrt(v + eps)

def _scatter_add(tgt, idx, src, axis=0):
    return tgt.at[idx].add(src)

def _segment_sum(src, seg, n):
    return jax.ops.segment_sum(src, seg, n)
kernel_name = 'mk_seq_preln_d2_jaxref_r8_b62da5'

def setup_inputs(seed: int=0):
    np.random.seed(seed)
    _w = jnp.asarray

    def _L0_attn_setup():
        import jax, jax.numpy as jnp
        import numpy as np
        B, T, C = (4, 512, 256)

        def _scan_op(a, bb):
            g_i, v_i = a
            g_j, v_j = bb
            return (g_j * g_i, g_j * v_i + v_j)
        key = jax.random.key(seed)
        k1, k2 = jax.random.split(key)
        x = jax.random.normal(k1, (B, T, C), dtype=jnp.float32)
        W = jax.random.normal(k2, (2 * C, C), dtype=jnp.float32) * (1.0 / np.sqrt(C))
        b = jnp.zeros((2 * C,), dtype=jnp.float32)
        return {'x': x, 'W': W, 'b': b}
    _L0_attn_in = _L0_attn_setup()

    def _L0_ffn_setup():
        import jax, jax.numpy as jnp
        import numpy as np
        B, T, C = (2, 128, 256)
        E, TOPK = (8, 2)
        F_MOE = 176
        F_SHARED = 704
        key = jax.random.key(seed)
        ks = jax.random.split(key, 9)
        s = 0.02
        return {'x': jax.random.normal(ks[0], (B, T, C), dtype=jnp.float32), 'gate_w': jax.random.normal(ks[1], (E, C), dtype=jnp.float32) * s, 'expert_fc1': jax.random.normal(ks[2], (E, F_MOE, C), dtype=jnp.float32) * s, 'expert_fc2': jax.random.normal(ks[3], (E, F_MOE, C), dtype=jnp.float32) * s, 'expert_proj': jax.random.normal(ks[4], (E, C, F_MOE), dtype=jnp.float32) * s, 'shared_fc1': jax.random.normal(ks[5], (F_SHARED, C), dtype=jnp.float32) * s, 'shared_fc2': jax.random.normal(ks[6], (F_SHARED, C), dtype=jnp.float32) * s, 'shared_proj': jax.random.normal(ks[7], (C, F_SHARED), dtype=jnp.float32) * s, 'shared_gate_w': jax.random.normal(ks[8], (1, C), dtype=jnp.float32) * s}
    _L0_ffn_in = _L0_ffn_setup()

    def _L1_attn_setup():
        import jax, jax.numpy as jnp
        import numpy as np
        B, S, D, H = (2, 256, 256, 16)
        HD = D // H
        key = jax.random.key(seed)
        ks = jax.random.split(key, 5)
        scale = 1.0 / np.sqrt(D)
        return {'x': jax.random.normal(ks[0], (B, S, D), dtype=jnp.float32), 'Wq': jax.random.normal(ks[1], (D, D), dtype=jnp.float32) * scale, 'Wk': jax.random.normal(ks[2], (D, D), dtype=jnp.float32) * scale, 'Wv': jax.random.normal(ks[3], (D, D), dtype=jnp.float32) * scale, 'Wo': jax.random.normal(ks[4], (D, D), dtype=jnp.float32) * scale}
    _L1_attn_in = _L1_attn_setup()

    def _L1_ffn_setup():
        import jax, jax.numpy as jnp
        import numpy as np
        D_MODEL = 256
        D_FF = 1024

        def absmean_quant(w):
            scale = jnp.mean(jnp.abs(w))
            mask = (jnp.abs(w) >= scale * 0.7).astype(w.dtype)
            return jnp.sign(w) * mask
        key = jax.random.key(seed)
        k_x, k_w1, k_w2 = jax.random.split(key, 3)
        x = jax.random.normal(k_x, (4, 512, D_MODEL), dtype=jnp.float32)
        w1 = jax.random.normal(k_w1, (D_FF, D_MODEL), dtype=jnp.float32)
        b1 = jnp.zeros((D_FF,), dtype=jnp.float32)
        w2 = jax.random.normal(k_w2, (D_MODEL, D_FF), dtype=jnp.float32)
        b2 = jnp.zeros((D_MODEL,), dtype=jnp.float32)
        return {'x': x, 'w1': w1, 'b1': b1, 'w2': w2, 'b2': b2}
    _L1_ffn_in = _L1_ffn_setup()
    _d = {'L0_attn_x': _L0_attn_in['x'], 'L0_attn_W': _L0_attn_in['W'], 'L0_attn_b': _L0_attn_in['b'], 'L0_ffn_gate_w': _L0_ffn_in['gate_w'], 'L0_ffn_expert_fc1': _L0_ffn_in['expert_fc1'], 'L0_ffn_expert_fc2': _L0_ffn_in['expert_fc2'], 'L0_ffn_expert_proj': _L0_ffn_in['expert_proj'], 'L0_ffn_shared_fc1': _L0_ffn_in['shared_fc1'], 'L0_ffn_shared_fc2': _L0_ffn_in['shared_fc2'], 'L0_ffn_shared_proj': _L0_ffn_in['shared_proj'], 'L0_ffn_shared_gate_w': _L0_ffn_in['shared_gate_w'], 'L1_attn_Wq': _L1_attn_in['Wq'], 'L1_attn_Wk': _L1_attn_in['Wk'], 'L1_attn_Wv': _L1_attn_in['Wv'], 'L1_attn_Wo': _L1_attn_in['Wo'], 'L1_ffn_w1': _L1_ffn_in['w1'], 'L1_ffn_b1': _L1_ffn_in['b1'], 'L1_ffn_w2': _L1_ffn_in['w2'], 'L1_ffn_b2': _L1_ffn_in['b2']}
    _x0 = _d['L0_attn_x']
    _d['L0_attn_x'] = jax.random.normal(jax.random.fold_in(jax.random.key(seed), 1), (4, 512, 256), dtype=_x0.dtype)
    del _x0
    return _d

def reference(L0_attn_x, L0_attn_W, L0_attn_b, L0_ffn_gate_w, L0_ffn_expert_fc1, L0_ffn_expert_fc2, L0_ffn_expert_proj, L0_ffn_shared_fc1, L0_ffn_shared_fc2, L0_ffn_shared_proj, L0_ffn_shared_gate_w, L1_attn_Wq, L1_attn_Wk, L1_attn_Wv, L1_attn_Wo, L1_ffn_w1, L1_ffn_b1, L1_ffn_w2, L1_ffn_b2):

    def _L0_attn_ref(x, W, b):
        import jax, jax.numpy as jnp
        import numpy as np
        B, T, C = (4, 512, 256)

        def _scan_op(a, bb):
            g_i, v_i = a
            g_j, v_j = bb
            return (g_j * g_i, g_j * v_i + v_j)
        params = jnp.einsum('btc,dc->btd', x, W) + b
        gates, values = jnp.split(params, 2, axis=-1)
        gates = jax.nn.sigmoid(gates)
        values = jnp.tanh(values)
        _, hidden = jax.lax.associative_scan(_scan_op, (gates, values), axis=1)
        return hidden

    def _L0_ffn_ref(x, gate_w, expert_fc1, expert_fc2, expert_proj, shared_fc1, shared_fc2, shared_proj, shared_gate_w):
        import jax, jax.numpy as jnp
        import numpy as np
        B, T, C = (2, 128, 256)
        E, TOPK = (8, 2)
        F_MOE = 176
        F_SHARED = 704
        b, t, c = x.shape
        xf = x.reshape(-1, c)
        n = xf.shape[0]
        router = xf @ gate_w.T
        probs = jax.nn.softmax(router.astype(jnp.float32), axis=1).astype(x.dtype)
        top_p, top_i = jax.lax.top_k(probs, TOPK)
        combine = jnp.zeros((n, E), dtype=x.dtype).at[jnp.arange(n)[:, None], top_i].set(top_p)
        h1 = jnp.einsum('nc,efc->enf', xf, expert_fc1)
        h2 = jnp.einsum('nc,efc->enf', xf, expert_fc2)
        h = jax.nn.silu(h1) * h2
        out_e = jnp.einsum('enf,ecf->enc', h, expert_proj)
        y = jnp.einsum('ne,enc->nc', combine, out_e)
        s1 = xf @ shared_fc1.T
        s2 = xf @ shared_fc2.T
        shared = jax.nn.silu(s1) * s2 @ shared_proj.T
        y = y + jax.nn.sigmoid(xf @ shared_gate_w.T) * shared
        return y.reshape(b, t, c)

    def _L1_attn_ref(x, Wq, Wk, Wv, Wo):
        import jax, jax.numpy as jnp
        import numpy as np
        B, S, D, H = (2, 256, 256, 16)
        HD = D // H
        b, s, d = x.shape

        def split_heads(t):
            return t.reshape(b, s, H, HD).transpose(0, 2, 1, 3)
        q = split_heads(x @ Wq.T)
        k = split_heads(x @ Wk.T)
        v = split_heads(x @ Wv.T)
        scores = jnp.einsum('bhqd,bhkd->bhqk', q, k) / jnp.sqrt(jnp.float32(HD))
        attn = jax.nn.softmax(scores, axis=-1)
        out = jnp.einsum('bhqk,bhkd->bhqd', attn, v)
        out = out.transpose(0, 2, 1, 3).reshape(b, s, d)
        return out @ Wo.T

    def _L1_ffn_ref(x, w1, b1, w2, b2):
        import jax, jax.numpy as jnp
        import numpy as np
        D_MODEL = 256
        D_FF = 1024

        def absmean_quant(w):
            scale = jnp.mean(jnp.abs(w))
            mask = (jnp.abs(w) >= scale * 0.7).astype(w.dtype)
            return jnp.sign(w) * mask
        w1_q = absmean_quant(w1)
        w2_q = absmean_quant(w2)
        h = jnp.einsum('bsd,fd->bsf', x, w1_q) + b1
        h = jax.nn.gelu(h, approximate=False)
        out = jnp.einsum('bsf,df->bsd', h, w2_q) + b2
        return out
    x = L0_attn_x
    x = x + _L0_attn_ref(_layernorm(x, axis=-1), L0_attn_W, L0_attn_b)
    x = x + _L0_ffn_ref(_layernorm(x, axis=-1), L0_ffn_gate_w, L0_ffn_expert_fc1, L0_ffn_expert_fc2, L0_ffn_expert_proj, L0_ffn_shared_fc1, L0_ffn_shared_fc2, L0_ffn_shared_proj, L0_ffn_shared_gate_w)
    x = x + _L1_attn_ref(_layernorm(x, axis=-1), L1_attn_Wq, L1_attn_Wk, L1_attn_Wv, L1_attn_Wo)
    x = x + _L1_ffn_ref(_layernorm(x, axis=-1), L1_ffn_w1, L1_ffn_b1, L1_ffn_w2, L1_ffn_b2)
    return x

_drawn_inputs = setup_inputs


def setup_inputs(seed=0):
    import zlib

    import numpy as np

    out = dict(_drawn_inputs(seed))
    spreads = {'L0_attn_b': (0.0, 0.1), 'L1_ffn_b1': (0.0, 0.8), 'L1_ffn_b2': (0.0, 2.0)}
    factors = {'L0_ffn_gate_w': 8.0,
     'L0_ffn_expert_fc1': 8.0,
     'L0_ffn_expert_fc2': 8.0,
     'L0_ffn_expert_proj': 8.0,
     'L0_ffn_shared_fc1': 5.214,
     'L0_ffn_shared_fc2': 5.204,
     'L0_ffn_shared_proj': 5.204,
     'L0_ffn_shared_gate_w': 8.0,
     'L1_attn_Wq': 4.283,
     'L1_attn_Wk': 4.242,
     'L1_attn_Wv': 3.415,
     'L1_attn_Wo': 3.384}
    for name, (base, spread) in spreads.items():
        noise = np.random.default_rng([zlib.crc32(name.encode()), seed]).standard_normal(out[name].shape)
        drawn = base * np.exp(spread * noise) if base else spread * noise
        out[name] = jnp.asarray(drawn.astype(out[name].dtype))
    for name, factor in factors.items():
        out[name] = (out[name] * factor).astype(out[name].dtype)
    return out
```

```python
import concourse.bass as bass
from concourse import mybir
from contextlib import ExitStack

B, T, C = 4, 512, 256
P = 128
CT = C // P
TT = T // P
NE, TOPK = 8, 2
FE, FS = 176, 704
F = NE * FE + FS
FC = -(-F // P)
NG = NE + 1
H, HD = 16, 16
HG = 4
GR = H // HG
DFF = 1024
DC = DFF // P
EPS = 1e-5
PAIRS = B // 2
LAG = 4
QPART, KPART = (0, 0, 1, 1, 0, 2), (0, 1, 0, 1, 2, 0)
KROWS = HD * len(QPART)
MROWS = KROWS + 3


def width(j):
    return min(P, F - j * P)


def build(nc, x, w0, b0, fc1, fc2, proj, gate, sel, wq, wk, wv, wo, w1, b1, w2, b2,
          ident, identb, sumsel, lower, out):
    f32, bf16 = mybir.dt.float32, mybir.dt.bfloat16
    ALU, ACT, AX = mybir.AluOpType, mybir.ActivationFunctionType, mybir.AxisListType

    ctx = ExitStack()
    with ctx:
        def sb(name, shape, dt):
            return ctx.enter_context(nc.sbuf_tensor(name, shape, dt))

        def sem(name):
            return ctx.enter_context(nc.semaphore(name))

        X = sb("X", [P, B * TT, C], f32)
        XN = sb("XN", [P, 2, TT, C], f32)
        XNT = sb("XNT", [P, 2, CT, T], f32)
        STATS = sb("STATS", [P, 2, TT, 6], f32)
        MV = sb("MV", [P, 2, TT, 2], f32)
        VE = sb("VE", [P, 2, TT], f32)
        RSTD = sb("RSTD", [P, 2, TT], f32)
        MHALF = sb("MHALF", [P, TT], f32)
        IDENT = sb("IDENT", [P, P], f32)
        IDENTB = sb("IDENTB", [P, P], bf16)
        SUMSEL = sb("SUMSEL", [P, P], f32)
        LOWER = sb("LOWER", [P, NE, NE], f32)
        ONES = sb("ONES", [P, P], f32)
        SEL = sb("SEL", [3 * NG, F], bf16)
        B0 = sb("B0", [P, 4], f32)
        GATE = sb("GATE", [P, CT, NG], f32)
        WQ = sb("WQ", [P, CT, C], f32)
        WK = sb("WK", [P, CT, C], f32)
        WV = sb("WV", [P, CT, C], f32)
        WO = sb("WO", [P, GR, C], f32)
        B1 = sb("B1", [P, DC], f32)
        B2 = sb("B2", [P, C], f32)
        W1Q = sb("W1Q", [P, CT, DFF], bf16)
        W2Q = sb("W2Q", [P, DC, C], bf16)

        BIG = sb("BIG", [P, 4 * H * T // 2], f32)
        FC1 = BIG[:, 0:CT * F].rearrange("p (k f) -> p k f", k=CT)
        FC2 = BIG[:, CT * F:2 * CT * F].rearrange("p (k f) -> p k f", k=CT)
        PROJ = BIG[:, 2 * CT * F:2 * CT * F + FC * C].rearrange("p (j c) -> p j c", j=FC)
        STACK = BIG[:].bitcast(bf16).rearrange("p (s h t) -> p s h t", s=4, h=H)
        QS = [STACK[:, p] for p in range(2)]
        KS = [STACK[:, 2 + p] for p in range(2)]

        WORKA = sb("WORKA", [P, 12 * T], f32)
        GV = WORKA[:, 0:8 * T].rearrange("p (b m t) -> p b m t", b=2, m=4)
        HS = WORKA[:, 8 * T:12 * T].rearrange("p (b m t) -> p b m t", b=2, m=CT)
        SILU = WORKA[:, 0:2 * T].rearrange("p (r t) -> p r t", r=2)
        UP = WORKA[:, 2 * T:8 * T].rearrange("p (r t) -> p r t", r=6)
        HID = WORKA[:, 8 * T:11 * T].rearrange("p (r t) -> p r t", r=3)
        PR = WORKA[:, 0:8 * T].rearrange("p (r h t) -> p r h t", r=2, h=HG)
        WORKB = sb("WORKB", [P, 8 * T], f32)
        RAW1 = WORKB[:, 0:4 * T].rearrange("p (k f) -> p k f", k=CT)
        RAW2 = WORKB[:, 4 * T:8 * T].rearrange("p (k f) -> p k f", k=DC)
        VA = WORKB[:, :].rearrange("p (b t h d) -> p b t h d", b=2, t=TT, h=H)
        WORKC = sb("WORKC", [P, 16 * T], f32)
        W0 = WORKC[:, 14 * T:16 * T].rearrange("p (k f) -> p k f", k=CT)
        QP = WORKC[:, 0:6 * T].bitcast(bf16).rearrange("p (w n t) -> p w n t", w=4, n=3)
        REST = WORKC[:, 6 * T:8 * T].rearrange("p (r t) -> p r t", r=2)
        U = WORKC[:, 8 * T:10 * T].rearrange("p (r t) -> p r t", r=2)
        RECIP = WORKC[:, 10 * T:11 * T]
        OT = WORKC[:, 11 * T:15 * T].rearrange("p (g t) -> p g t", g=GR)
        NT = WORKC[:, 15 * T:16 * T].bitcast(bf16).rearrange("p (r t) -> p r t", r=2)
        QTMP = WORKC[:, 0:4 * T]
        XR = WORKC[:, 0:4 * T].rearrange("p (b k t) -> p b k t", b=2, k=CT)
        X3 = WORKC[:, 4 * T:6 * T].bitcast(bf16).rearrange("p (b k t) -> p b k t", b=2, k=CT)
        GE = WORKC[:, 6 * T:9 * T].rearrange("p (r t) -> p r t", r=3)
        GREM = WORKC[:, 9 * T:12 * T].rearrange("p (r t) -> p r t", r=3)
        G3 = WORKC[:, 12 * T:12 * T + 3 * T // 2].bitcast(bf16).rearrange("p (r t) -> p r t", r=3)

        LOGIT = sb("LOGIT", [NG, T], f32)
        ROWMAX = sb("ROWMAX", [P, TT], f32)
        ZE = sb("ZE", [P, TT, NE], f32)
        ZS = sb("ZS", [P, TT], f32)
        EE = sb("EE", [P, TT, NE], f32)
        ES = sb("ES", [P, TT], f32)
        ESUM = sb("ESUM", [P, TT], f32)
        ERCP = sb("ERCP", [P, TT], f32)
        GT = sb("GT", [P, TT, NE, NE], f32)
        EQ = sb("EQ", [P, TT, NE, NE], f32)
        RANK = sb("RANK", [P, TT, NE], f32)
        SELE = sb("SELE", [P, TT, NE], f32)
        COMB = sb("COMB", [P, TT, NG], f32)
        CREM = sb("CREM", [P, TT, NG], f32)
        CPART = sb("CPART", [P, TT, 3, NG], bf16)
        COMBT = sb("COMBT", [3 * NG, 2, T], bf16)
        MX = sb("MX", [P, 2, H, TT], f32)
        NREM = sb("NREM", [P, HG, TT], f32)
        NP = sb("NP", [P, 2, TT, 3, HG], bf16)
        WSUM = sb("WSUM", [P, 2], f32)
        WMEAN = sb("WMEAN", [P, 2], f32)
        THR = sb("THR", [P, 2], f32)
        NTHR = sb("NTHR", [P, 2], f32)

        PS = ctx.enter_context(nc.psum_tensor("PS", [P, 8, 512], f32))
        MISC = PS[:, 7]
        MISCB = MISC.bitcast(bf16)

        qk_dram = nc.dram_tensor("qk_parts", [B, 4, 3, P, T], bf16, kind="Internal").ap()
        nm_dram = nc.dram_tensor("neg_max_parts", [B, GR, 3 * HG, T], bf16, kind="Internal").ap()

        held = sem("held")
        x_first, x_rest = sem("x_first"), sem("x_rest")
        w0_in, ident_in, const_in, mix_in, attn_in, ffn_in = (sem(n) for n in (
            "w0_in", "ident_in", "const_in", "mix_in", "attn_in", "ffn_in"))
        ones_set, half_set = sem("ones_set"), sem("half_set")
        ln_stats, ln_mv, ln_pool, xn_ready, xnt_psum, xnt_ready = (sem(n) for n in (
            "ln_stats", "ln_mv", "ln_pool", "xn_ready", "xnt_psum", "xnt_ready"))
        scan_mm, scan_act, scanned, back_mm, resid_a = (sem(n) for n in (
            "scan_mm", "scan_act", "scanned", "back_mm", "resid_a"))
        (logit_mm, logit_sb, logit_t, router_step, comb_step, router_z, router_e, comb_mm, comb_ready,
         h1_mm, h2_mm, silu_ready, up_ready, c_mm, hid_ready, y_part, resid_b) = (sem(n) for n in (
            "logit_mm", "logit_sb", "logit_t", "router_step", "comb_step", "router_z", "router_e", "comb_mm",
            "comb_ready", "h1_mm", "h2_mm", "silu_ready", "up_ready", "c_mm", "hid_ready",
            "y_part", "resid_b"))
        wabs, wtot, wstep, tern_ready = (sem(n) for n in ("wabs", "wtot", "wstep", "tern_ready"))
        (q_mm, q_part1, q_rest, q_part2, q_part3, v_mm, v_ready, k_ones, v_ones, top_mm, top_ready,
         neg_step, neg_t, nt_ready, s_mm, exp_done, pv_done, u_ready, sum_mm, rc_ready, o_ready,
         wo_mm, resid_c) = (sem(n) for n in (
            "q_mm", "q_part1", "q_rest", "q_part2", "q_part3", "v_mm", "v_ready", "k_ones", "v_ones",
            "top_mm", "top_ready", "neg_step", "neg_t", "nt_ready", "s_mm", "exp_done", "pv_done",
            "u_ready", "sum_mm", "rc_ready", "o_ready", "wo_mm", "resid_c"))
        parts_out = [sem(f"parts_out{w}") for w in range(4)]
        stack_in = [sem(f"stack_in{p}") for p in range(2)]
        nm_out = [sem(f"nm_out{g}") for g in range(GR)]
        nm_in = [sem(f"nm_in{g}") for g in range(GR)]
        (x_rem, x_part3, ff_mm, ge_ready, g_rem, g_part3, yf_part, b2_added, resid_d, stored) = (
            sem(n) for n in ("x_rem", "x_part3", "ff_mm", "ge_ready", "g_rem", "g_part3", "yf_part",
                             "b2_added", "resid_d", "stored"))

        CREDIT = {scan_act: 4, resid_a: 2, silu_ready: 2, up_ready: 2, hid_ready: 1, y_part: 3,
                  resid_b: 2, q_rest: 4, q_part3: 2, top_ready: 2, exp_done: 2, pv_done: 2, v_ready: 2,
                  u_ready: 1, o_ready: 2, resid_c: 2, ge_ready: 2, yf_part: 3, resid_d: 2}
        for w in range(4):
            CREDIT[parts_out[w]] = 16
            CREDIT[nm_out[w]] = 16

        def need(eng, s, n):
            eng.wait_ge(s, n + CREDIT.get(s, 0))

        def hold(eng, s, n):
            need(eng, s, n)
            eng.sem_inc(held, 1)

        def batches(eng):
            with eng.Fori(0, PAIRS) as i:
                for p in range(2):
                    yield 2 * i + p, p

        def following(b, p):
            return b + 1 if p == 0 else B - 1 - b

        def tiles(b, j=0, n=TT):
            return bass.ds(TT * b + j, n)

        def y_bank(j):
            return PS[:, 5 + j].rearrange("p (t c) -> p t c", t=2)

        def ln_stats_of(dve, n, q, src):
            for t in range(TT):
                nc.vector.bn_stats(STATS[:, q, t], X[:, bass.ds(src * TT + t, 1)]).then_inc(ln_stats, 1)
            hold(dve, ln_stats, 4 * n + 4)
            for t in range(TT):
                nc.vector.bn_aggr(MV[:, q, t], STATS[:, q, t]).then_inc(ln_mv, 1)

        def ln_apply(pool, n, q, src):
            hold(pool, ln_mv, 4 * n + 4)
            nc.gpsimd.tensor_scalar(VE[:, q], MV[:, q, :, 1], EPS, None, ALU.add).then_inc(ln_pool, 1)
            hold(pool, ln_pool, 3 * n + 1)
            nc.gpsimd.tensor_tensor(RSTD[:, q], VE[:, q], MHALF[:], ALU.pow).then_inc(ln_pool, 1)
            mean = MV[:, q, :, 0].unsqueeze(2).broadcast_to([P, TT, C])
            nc.gpsimd.tensor_tensor(XN[:, q], X[:, tiles(src)], mean, ALU.subtract).then_inc(ln_pool, 1)
            hold(pool, ln_pool, 3 * n + 3)
            nc.gpsimd.tensor_tensor(XN[:, q], XN[:, q], RSTD[:, q].unsqueeze(2).broadcast_to([P, TT, C]),
                                    ALU.mult).then_inc(xn_ready, 1)

        def ln_transpose(pe, n, q, c):
            pe.wait_ge(xn_ready, n + 1)
            if c == 1:
                pe.wait_ge(xnt_ready, 2 * n + 1)
            for t in range(TT):
                mm = nc.tensor.transpose(MISC[:, t * P:(t + 1) * P], XN[:, q, t, c * P:(c + 1) * P], IDENT[:])
            mm.then_inc(xnt_psum, 1)

        def ln_copy(act, n, q, c):
            act.wait_ge(xnt_psum, 2 * n + c + 1)
            nc.scalar.activation(XNT[:, q, c], MISC, ACT.Copy).then_inc(xnt_ready, 1)

        block = ctx.enter_context(nc.Block())

        @block.sync
        def _(sp):
            for s, n in CREDIT.items():
                sp.sem_inc(s, n)
            xt = x.rearrange("b (t p) c -> b p t c", p=P)
            sp.dma_start(X[:, 0:TT], xt[0]).then_inc(x_first, 16)
            sp.dma_start(IDENT[:], ident).then_inc(ident_in, 16)
            sp.dma_start(W0, w0).then_inc(w0_in, 16)
            sp.dma_start(B0[:], b0).then_inc(w0_in, 16)
            for b in range(1, B):
                sp.dma_start(X[:, b * TT:(b + 1) * TT], xt[b]).then_inc(x_rest, 16)
            for dst, src in ((IDENTB, identb), (SUMSEL, sumsel), (LOWER, lower), (SEL, sel)):
                sp.dma_start(dst[:], src).then_inc(const_in, 16)
            for dst, src in ((GATE[:], gate), (FC1, fc1), (FC2, fc2), (PROJ, proj)):
                sp.dma_start(dst, src).then_inc(mix_in, 16)
            for dst, src in ((RAW1, w1), (RAW2, w2), (B1[:], b1), (B2[:], b2)):
                sp.dma_start(dst, src).then_inc(ffn_in, 16)
            for dst, src in ((WQ, wq), (WK, wk), (WV, wv), (WO, wo)):
                sp.dma_start(dst[:], src).then_inc(attn_in, 16)

            def parts(b, w, q):
                need(sp, q_part3, 4 * b + w + 1)
                sp.dma_start(qk_dram[bass.ds(b, 1), w].rearrange("a n p t -> p (a n) t"),
                             QP[:, w]).then_inc(parts_out[w], 16)

            def stack(b, w, q):
                need(sp, parts_out[w], 16 * b + 16)
                part = (QPART, KPART)[w // 2]
                dst = (QS, KS)[w // 2][q]
                h0 = (w % 2) * (H // 2)
                for g, n in enumerate(part):
                    sp.dma_start(dst[HD * g:HD * (g + 1), h0:h0 + H // 2],
                                 qk_dram[bass.ds(b, 1), w, n].rearrange("a (h d) t -> d (a h) t", d=HD)
                                 ).then_inc(stack_in[q], 16)

            def neg_rows(b, g, q):
                sp.wait_ge(nt_ready, 4 * b + g + 1)
                sp.dma_start(nm_dram[bass.ds(b, 1), g].rearrange("a r t -> (a r) t"),
                             NT[0:3 * HG, g % 2]).then_inc(nm_out[g], 16)
                need(sp, nm_out[g], 16 * b + 16)
                sp.dma_start(QS[q][KROWS:MROWS, HG * g:HG * (g + 1)],
                             nm_dram[bass.ds(b, 1), g].rearrange("a (n h) t -> (a n) h t", n=3)
                             ).then_inc(nm_in[g], 16)

            with sp.Fori(0, PAIRS) as i:
                for p in range(2):
                    for w in range(4):
                        parts(2 * i + p, w, p)
                    for w in range(4):
                        stack(2 * i + p, w, p)
                for p in range(2):
                    for g in range(GR):
                        neg_rows(2 * i + p, g, p)
            ot = out.rearrange("b (t p) c -> b p t c", p=P)
            with sp.Fori(0, B) as b:
                need(sp, resid_d, 2 * b + 2)
                sp.dma_start(ot[bass.ds(b, 1)].rearrange("a p t c -> p (a t) c"),
                             X[:, tiles(b)]).then_inc(stored, 16)
            sp.wait_ge(stored, 16 * B)

        @block.gpsimd
        def _(pool):
            nc.gpsimd.memset(MHALF[:], -0.5).then_inc(half_set, 1)
            nc.gpsimd.memset(ONES[:], 1.0).then_inc(ones_set, 1)
            pool.wait_ge(half_set, 1)
            ln_apply(pool, 0, 0, 0)
            for stage in range(2):
                for b, p in batches(pool):
                    ln_apply(pool, 4 * stage + b + 1, 1 - p, following(b, p))
            need(pool, resid_b, 2 * B)
            for p in range(2):
                nc.gpsimd.memset(KS[p][KROWS:MROWS], 1.0).then_inc(k_ones, 1)
                pool.wait_ge(k_ones, p + 1)
            for p in range(2):
                nc.gpsimd.memset(VA[:, p, :, :, HD:2 * HD], 1.0).then_inc(v_ones, 1)

            def q_parts(b, w):
                pool.wait_ge(q_part1, 4 * b + w + 1)
                hold(pool, q_rest, 4 * b + w + 1)
                nc.gpsimd.tensor_copy(QP[:, w, 1], REST[:, w % 2]).then_inc(q_part2, 1)
                pool.wait_ge(q_part2, 4 * b + w + 1)
                nc.gpsimd.tensor_tensor(QP[:, w, 2], REST[:, w % 2], QP[:, w, 1],
                                        ALU.subtract).then_inc(q_part3, 1)

            with pool.Fori(0, PAIRS) as i:
                e, o = 2 * i, 2 * i + 1
                ln_apply(pool, 9 + e, 1, following(e, 0))
                for b in (e, o):
                    for w in range(4):
                        q_parts(b, w)
                ln_apply(pool, 9 + o, 0, following(o, 1))
            for b, p in batches(pool):
                for t in range(TT):
                    xt = X[:, bass.ds(TT * b + t, 1)].rearrange("p a c -> p (a c)")
                    nc.gpsimd.tensor_tensor(xt, xt, B2[:], ALU.add).then_inc(b2_added, 1)
                ln_apply(pool, 13 + b, 1 - p, following(b, p))
                for j in range(DC):
                    pool.wait_ge(g_rem, DC * b + j + 1)
                    need(pool, yf_part, DC * b + j - 2)
                    nc.gpsimd.tensor_tensor(G3[:, j % 3], GREM[:, j % 3],
                                            GREM[:, j % 3].bitcast(bf16)[:, 1:2 * T:2],
                                            ALU.subtract).then_inc(g_part3, 1)

        @block.scalar
        def _(act):
            for c in range(CT):
                ln_copy(act, 0, 0, c)
            act.wait_ge(w0_in, 32)
            for b, p in batches(act):
                for k, m in enumerate((0, 2, 1, 3)):
                    act.wait_ge(scan_mm, 4 * b + k + 1)
                    nc.scalar.activation(GV[:, p, m], PS[:, m], ACT.Sigmoid if m < 2 else ACT.Tanh,
                                         bias=B0[:, m:m + 1]).then_inc(scan_act, 1)
                for c in range(CT):
                    ln_copy(act, b + 1, 1 - p, c)
            act.wait_ge(ffn_in, 64)
            nc.scalar.activation(QTMP, RAW1.rearrange("p k f -> p (k f)"), ACT.Abs,
                                 accum_out=WSUM[:, 0:1]).then_inc(wabs, 1)
            act.wait_ge(wabs, 1)
            nc.scalar.activation(QTMP, RAW2.rearrange("p k f -> p (k f)"), ACT.Abs,
                                 accum_out=WSUM[:, 1:2]).then_inc(wabs, 1)
            for b, p in batches(act):
                act.wait_ge(logit_mm, b + 1)
                nc.scalar.activation(LOGIT[:], MISC[0:NG], ACT.Copy).then_inc(logit_sb, 1)
                for j in range(FC):
                    act.wait_ge(h1_mm, FC * b + j + 1)
                    need(act, up_ready, FC * b + j - 1)
                    nc.scalar.activation(SILU[0:width(j), j % 2], PS[0:width(j), j % 2],
                                         ACT.Silu).then_inc(silu_ready, 1)
                    if j == 0:
                        act.wait_ge(router_z, 2 * b + 2)
                        nc.scalar.activation(EE[:], ZE[:], ACT.Exp).then_inc(router_e, 1)
                        nc.scalar.activation(ES[:], ZS[:], ACT.Exp, scale=-1.0).then_inc(router_e, 1)
                    if j == 3:
                        act.wait_ge(comb_mm, b + 1)
                        nc.scalar.activation(COMBT[:, p], MISCB[0:3 * NG, 0:T], ACT.Copy).then_inc(comb_ready, 1)
                    if j in (8, 9):
                        ln_copy(act, 5 + b, 1 - p, j - 8)

            def part1(b, w):
                act.wait_ge(q_mm, 4 * b + w + 1)
                need(act, parts_out[w], 16 * b)
                nc.scalar.activation(QP[:, w, 0], PS[:, 2 + w], ACT.Copy).then_inc(q_part1, 1)

            def v_copy(b, q, j):
                act.wait_ge(v_mm, 2 * b + j + 1)
                nc.scalar.activation(VA[:, q, 2 * j:2 * j + 2, :, 0:HD],
                                     PS[:, j].rearrange("p (t h d) -> p t h d", t=2, h=H),
                                     ACT.Copy).then_inc(v_ready, 1)

            def nt_copy(b, g):
                act.wait_ge(neg_t, 4 * b + g + 1)
                need(act, nm_out[(g + 2) % GR], 16 * b + 16 * (g // 2))
                nc.scalar.activation(NT[0:3 * HG, g % 2], MISCB[0:3 * HG, 0:T], ACT.Copy).then_inc(nt_ready, 1)

            def exps(b, g, kt):
                for j in range(2):
                    act.wait_ge(s_mm, 32 * b + 8 * g + 2 * kt + j + 1)
                    if j == 0:
                        need(act, pv_done, 16 * b + 4 * g + kt - 1)
                    nc.scalar.activation(PR[:, kt % 2, 2 * j:2 * j + 2],
                                         PS[:, 2 + 2 * j:4 + 2 * j], ACT.Exp, scale=0.25).then_inc(exp_done, 1)

            def u_copy(b, g):
                need(act, pv_done, 16 * b + 4 * g + 4)
                need(act, o_ready, 4 * b + g - 1)
                nc.scalar.activation(U[:, g % 2], PS[:, 6], ACT.Copy).then_inc(u_ready, 1)

            act.wait_ge(v_ones, 2)
            with act.Fori(0, PAIRS) as i:
                e, o = 2 * i, 2 * i + 1
                for w in range(4):
                    part1(e, w)
                for j in range(2):
                    v_copy(e, 0, j)
                for c in range(CT):
                    ln_copy(act, 9 + e, 1, c)
                for w in range(4):
                    part1(o, w)
                for j in range(2):
                    v_copy(o, 1, j)
                for g in range(GR):
                    nt_copy(e, g)
                for s in range(4 * GR + 1):
                    g, kt = divmod(s, 4)
                    if s < 4 * GR:
                        exps(e, g, kt)
                    if kt == 0 and g:
                        u_copy(e, g - 1)
                    if kt == 1 and g:
                        nt_copy(o, g - 1)
                nt_copy(o, GR - 1)
                for c in range(CT):
                    ln_copy(act, 9 + o, 0, c)
                for s in range(4 * GR + 1):
                    g, kt = divmod(s, 4)
                    if s < 4 * GR:
                        exps(o, g, kt)
                    if kt == 0 and g:
                        u_copy(o, g - 1)
            for b, p in batches(act):
                for j in range(DC):
                    act.wait_ge(ff_mm, DC * b + j + 1)
                    need(act, yf_part, DC * b + j - 2)
                    nc.scalar.activation(GE[:, j % 3], PS[:, j % 2], ACT.Gelu,
                                         bias=B1[:, j:j + 1]).then_inc(ge_ready, 1)
                    if j in (5, 6):
                        ln_copy(act, 13 + b, 1 - p, j - 5)

        @block.vector
        def _(dve):
            dve.wait_ge(x_first, 16)
            ln_stats_of(dve, 0, 0, 0)
            dve.wait_ge(x_rest, 16 * (B - 1))
            for b, p in batches(dve):
                hold(dve, resid_a, 2 * b)
                ln_stats_of(dve, b + 1, 1 - p, following(b, p))
                for c in range(CT):
                    need(dve, scan_act, 4 * b + 2 * c + 2)
                    nc.vector.tensor_tensor_scan(HS[:, p, c], GV[:, p, c], GV[:, p, 2 + c], 0.0,
                                                 ALU.mult, ALU.add).then_inc(scanned, 1)
                for j in range(2):
                    dve.wait_ge(back_mm, 2 * b + j + 1)
                    xs = X[:, tiles(b, 2 * j, 2)]
                    nc.vector.tensor_tensor(xs, PS[:, 4 + j].rearrange("p (t c) -> p t c", t=2), xs,
                                            ALU.add).then_inc(resid_a, 1)
            dve.wait_ge(wtot, 1)
            nc.vector.tensor_scalar(WMEAN[:], MISC[:, 0:2], 1.0 / (C * DFF), None, ALU.mult).then_inc(wstep, 1)
            dve.wait_ge(wstep, 1)
            nc.vector.tensor_scalar(THR[:], WMEAN[:], 0.7, None, ALU.mult).then_inc(wstep, 1)
            dve.wait_ge(wstep, 2)
            nc.vector.tensor_scalar(NTHR[:], THR[:], -1.0, None, ALU.mult).then_inc(wstep, 1)
            dve.wait_ge(wstep, 3)
            for k, (raw, tern) in enumerate(((RAW1, W1Q), (RAW2, W2Q))):
                raw, tern = raw.rearrange("p k f -> p (k f)"), tern[:].rearrange("p k f -> p (k f)")
                if k:
                    dve.wait_ge(tern_ready, k)
                nc.vector.tensor_scalar(QTMP, raw, NTHR[:, k:k + 1], None, ALU.is_le).then_inc(wstep, 1)
                dve.wait_ge(wstep, 4 + k)
                nc.vector.scalar_tensor_tensor(tern, raw, THR[:, k:k + 1], QTMP,
                                               ALU.is_ge, ALU.subtract).then_inc(tern_ready, 1)

            RS = 13

            def router(b, k0, ops):
                for k, op in enumerate(ops, k0):
                    if k:
                        dve.wait_ge(router_step, RS * b + k)
                    op().then_inc(router_step, 1)

            V = nc.vector

            def bc_i(a):
                return a.unsqueeze(2).broadcast_to([P, TT, NE, NE])

            def bc_j(a):
                return a.unsqueeze(3).broadcast_to([P, TT, NE, NE])

            def bc_e(a, n=NE):
                return a.unsqueeze(2).broadcast_to([P, TT, n])

            LG = MISC[:, 0:16 * TT].rearrange("p (t e) -> p t e", t=TT)
            for b, p in batches(dve):
                hold(dve, resid_b, 2 * b)
                for j in range(FC + LAG):
                    if j < FC:
                        wd = width(j)
                        need(dve, silu_ready, FC * b + j + 1)
                        dve.wait_ge(h2_mm, FC * b + j + 1)
                        V.tensor_tensor(UP[0:wd, j % 6], PS[0:wd, 2 + j % 2], SILU[0:wd, j % 2],
                                        ALU.mult).then_inc(up_ready, 1)
                    if j == 0:
                        dve.wait_ge(logit_t, b + 1)
                        router(b, 0, [lambda: V.tensor_reduce(ROWMAX[:], LG[:, :, 0:NE], AX.X, ALU.max)])
                        dve.wait_ge(router_step, RS * b + 1)
                        V.tensor_tensor(ZE[:], LG[:, :, 0:NE], bc_e(ROWMAX[:]), ALU.subtract).then_inc(router_z, 1)
                        V.tensor_copy(ZS[:], LG[:, :, NE]).then_inc(router_z, 1)
                    if j == 1:
                        dve.wait_ge(router_e, 2 * b + 2)
                        router(b, 1, [
                            lambda: V.tensor_reduce(ESUM[:], EE[:], AX.X, ALU.add),
                            lambda: V.reciprocal(ERCP[:], ESUM[:]),
                            lambda: V.tensor_tensor(GT[:], bc_i(EE[:]), bc_j(EE[:]), ALU.is_gt),
                            lambda: V.tensor_tensor(EQ[:], bc_i(EE[:]), bc_j(EE[:]), ALU.is_equal),
                            lambda: V.tensor_tensor(EQ[:], EQ[:], LOWER[:].unsqueeze(1).broadcast_to(
                                [P, TT, NE, NE]), ALU.mult),
                            lambda: V.tensor_tensor(GT[:], GT[:], EQ[:], ALU.add),
                            lambda: V.tensor_reduce(RANK[:], GT[:], AX.X, ALU.add),
                            lambda: V.scalar_tensor_tensor(SELE[:], RANK[:], TOPK - 0.5, EE[:],
                                                           ALU.is_lt, ALU.mult),
                            lambda: V.tensor_tensor(COMB[:, :, 0:NE], SELE[:], bc_e(ERCP[:]), ALU.mult),
                            lambda: V.tensor_scalar(ESUM[:], ES[:], 1.0, None, ALU.add),
                            lambda: V.reciprocal(COMB[:, :, NE], ESUM[:]),
                            lambda: V.tensor_copy(CPART[:, :, 0], COMB[:]),
                        ])
                        assert RS == 13
                        dve.wait_ge(router_step, RS * b + RS)
                        V.tensor_tensor(CREM[:], COMB[:], CPART[:, :, 0], ALU.subtract).then_inc(comb_step, 1)
                        dve.wait_ge(comb_step, 3 * b + 1)
                        V.tensor_copy(CPART[:, :, 1], CREM[:]).then_inc(comb_step, 1)
                        dve.wait_ge(comb_step, 3 * b + 2)
                        V.tensor_tensor(CPART[:, :, 2], CREM[:], CPART[:, :, 1], ALU.subtract).then_inc(comb_step, 1)
                    if j == 4:
                        ln_stats_of(dve, 5 + b, 1 - p, following(b, p))
                    jw = j - LAG
                    if jw >= 0:
                        wd = width(jw)
                        dve.wait_ge(c_mm, FC * b + jw + 1)
                        need(dve, up_ready, FC * b + jw + 1)
                        need(dve, y_part, FC * b + jw - 2)
                        V.tensor_tensor(HID[0:wd, jw % 3], PS[0:wd, 4], UP[0:wd, jw % 6],
                                        ALU.mult).then_inc(hid_ready, 1)
                need(dve, y_part, FC * b + FC)
                for j in range(2):
                    xs = X[:, tiles(b, 2 * j, 2)]
                    V.tensor_tensor(xs, y_bank(j), xs, ALU.add).then_inc(resid_b, 1)

            def rest1(b, w):
                dve.wait_ge(q_part1, 4 * b + w + 1)
                need(dve, q_part3, 4 * b + w - 1)
                V.tensor_tensor(REST[:, w % 2], PS[:, 2 + w], QP[:, w, 0], ALU.subtract).then_inc(q_rest, 1)

            def top(b, q, k):
                dve.wait_ge(top_mm, 64 * b + k + 1)
                V.tensor_reduce(MX[:, q, k // TT, k % TT:k % TT + 1], PS[:, k % 2], AX.X, ALU.max
                                ).then_inc(top_ready, 1)

            def negate(b, q, g):
                need(dve, top_ready, 64 * b + 16 * g + 16)
                m = MX[:, q, HG * g:HG * (g + 1)]
                part = [NP[:, g % 2, :, n].rearrange("p t h -> p h t") for n in range(3)]
                k0 = 16 * b + 4 * g
                V.tensor_scalar(part[0], m, -1.0, None, ALU.mult).then_inc(neg_step, 1)
                dve.wait_ge(neg_step, k0 + 1)
                V.scalar_tensor_tensor(NREM[:], m, -1.0, part[0], ALU.mult, ALU.subtract).then_inc(neg_step, 1)
                dve.wait_ge(neg_step, k0 + 2)
                V.tensor_copy(part[1], NREM[:]).then_inc(neg_step, 1)
                dve.wait_ge(neg_step, k0 + 3)
                V.tensor_tensor(part[2], NREM[:], part[1], ALU.subtract).then_inc(neg_step, 1)

            def normalise(b, g):
                dve.wait_ge(sum_mm, 4 * b + g + 1)
                need(dve, o_ready, 4 * b + g)
                V.reciprocal(RECIP, MISC).then_inc(rc_ready, 1)
                dve.wait_ge(rc_ready, 4 * b + g + 1)
                V.tensor_tensor(OT[:, g], U[:, g % 2], RECIP, ALU.mult).then_inc(o_ready, 1)

            def add_c(b):
                for j in range(2):
                    dve.wait_ge(wo_mm, 2 * b + j + 1)
                    xs = X[:, tiles(b, 2 * j, 2)]
                    V.tensor_tensor(xs, MISC.rearrange("p (t c) -> p t c", t=2), xs, ALU.add
                                    ).then_inc(resid_c, 1)

            need(dve, resid_b, 2 * B)
            with dve.Fori(0, PAIRS) as i:
                e, o = 2 * i, 2 * i + 1
                ln_stats_of(dve, 9 + e, 1, following(e, 0))
                for b in (e, o):
                    for w in range(4):
                        rest1(b, w)
                for g in range(GR):
                    for k in range(16):
                        top(e, 0, 16 * g + k)
                    negate(e, 0, g)
                for s in range(4 * GR):
                    g, kt = divmod(s, 4)
                    for k in range(4):
                        top(o, 1, 4 * s + k)
                    if kt == 1 and g:
                        normalise(e, g - 1)
                    if kt == 3:
                        negate(o, 1, g)
                normalise(e, GR - 1)
                add_c(e)
                hold(dve, resid_c, 2 * e)
                ln_stats_of(dve, 9 + o, 0, following(o, 1))
                for g in range(GR):
                    normalise(o, g)
                add_c(o)

            def x_parts(b, q):
                dve.wait_ge(xnt_ready, 2 * b + 26)
                V.tensor_tensor(XR[:, q], XNT[:, q], XNT[:, q].bitcast(bf16)[:, :, 1:2 * T:2],
                                ALU.subtract).then_inc(x_rem, 1)
                dve.wait_ge(x_rem, b + 1)
                V.tensor_tensor(X3[:, q], XR[:, q], XR[:, q].bitcast(bf16)[:, :, 1:2 * T:2],
                                ALU.subtract).then_inc(x_part3, 1)

            need(dve, resid_c, 2 * B)
            x_parts(0, 0)
            for b, p in batches(dve):
                hold(dve, resid_d, 2 * b)
                for j in range(DC):
                    need(dve, ge_ready, DC * b + j + 1)
                    need(dve, yf_part, DC * b + j - 2)
                    V.tensor_tensor(GREM[:, j % 3], GE[:, j % 3], GE[:, j % 3].bitcast(bf16)[:, 1:2 * T:2],
                                    ALU.subtract).then_inc(g_rem, 1)
                    if j == 1:
                        ln_stats_of(dve, 13 + b, 1 - p, following(b, p))
                x_parts(b + 1, 1 - p)
                need(dve, yf_part, DC * b + DC)
                dve.wait_ge(b2_added, TT * b + TT)
                for j in range(2):
                    xs = X[:, tiles(b, 2 * j, 2)]
                    V.tensor_tensor(xs, y_bank(j), xs, ALU.add).then_inc(resid_d, 1)

        @block.tensor
        def _(pe):
            MM = nc.tensor.matmul
            pe.wait_ge(ident_in, 16)
            for c in range(CT):
                ln_transpose(pe, 0, 0, c)
            pe.wait_ge(w0_in, 32)
            for b, p in batches(pe):
                pe.wait_ge(xnt_ready, 2 * b + 2)
                for k, m in enumerate((0, 2, 1, 3)):
                    need(pe, scan_act, 4 * b + k - 3)
                    for c in range(CT):
                        mm = MM(PS[:, m], W0[:, c, m * P:(m + 1) * P], XNT[:, p, c], start=c == 0, stop=c == CT - 1)
                    mm.then_inc(scan_mm, 1)
                for c in range(CT):
                    ln_transpose(pe, b + 1, 1 - p, c)
                pe.wait_ge(scanned, 2 * b + 2)
                need(pe, resid_a, 2 * b)
                for t in range(TT):
                    for c in range(CT):
                        mm = nc.tensor.transpose(PS[:, 4 + t // 2, (t % 2) * C + c * P:(t % 2) * C + (c + 1) * P],
                                                 HS[:, p, c, t * P:(t + 1) * P], IDENT[:])
                    if t % 2:
                        mm.then_inc(back_mm, 1)
            pe.wait_ge(wabs, 2)
            pe.wait_ge(ones_set, 1)
            pe.wait_ge(xnt_ready, 10)
            MM(MISC[:, 0:2], ONES[:], WSUM[:], start=True, stop=True).then_inc(wtot, 1)
            pe.wait_ge(mix_in, 64)
            pe.wait_ge(const_in, 64)
            pe.wait_ge(tern_ready, 2)
            for b, p in batches(pe):
                pe.wait_ge(xnt_ready, 2 * b + 10)
                for c in range(CT):
                    mm = MM(MISC[0:NG], GATE[:, c], XNT[:, p, c], start=c == 0, stop=c == CT - 1)
                mm.then_inc(logit_mm, 1)
                for j in range(FC + LAG + 1):
                    if j < FC:
                        wd = width(j)
                        need(pe, silu_ready, FC * b + j - 1)
                        for c in range(CT):
                            mm = MM(PS[0:wd, j % 2], FC1[:, c, j * P:j * P + wd], XNT[:, p, c],
                                    start=c == 0, stop=c == CT - 1)
                        mm.then_inc(h1_mm, 1)
                        need(pe, up_ready, FC * b + j - 1)
                        for c in range(CT):
                            mm = MM(PS[0:wd, 2 + j % 2], FC2[:, c, j * P:j * P + wd], XNT[:, p, c],
                                    start=c == 0, stop=c == CT - 1)
                        mm.then_inc(h2_mm, 1)
                    if j == 0:
                        hold(pe, logit_sb, b + 1)
                        for t in range(TT):
                            mm = nc.tensor.transpose(MISC[:, 16 * t:16 * t + NG], LOGIT[:, t * P:(t + 1) * P],
                                                     IDENT[0:NG, 0:NG])
                        mm.then_inc(logit_t, 1)
                    if j == 2:
                        pe.wait_ge(comb_step, 3 * b + 3)
                        for t in range(TT):
                            mm = nc.tensor.transpose(MISCB[0:3 * NG, t * P:(t + 1) * P],
                                                     CPART[:, t].rearrange("p n e -> p (n e)"), IDENTB[:])
                        mm.then_inc(comb_mm, 1)
                    if j in (8, 9):
                        ln_transpose(pe, 5 + b, 1 - p, j - 8)
                    jc = j - LAG
                    if 0 <= jc < FC:
                        if jc == 0:
                            pe.wait_ge(comb_ready, b + 1)
                            need(pe, resid_a, 2 * B)
                        need(pe, hid_ready, FC * b + jc)
                        MM(PS[0:width(jc), 4], SEL[:, jc * P:jc * P + width(jc)], COMBT[:, p],
                           start=True, stop=True).then_inc(c_mm, 1)
                    jp = jc - 1
                    if jp >= 0:
                        wd = width(jp)
                        if jp == 0:
                            need(pe, resid_b, 2 * b)
                        need(pe, hid_ready, FC * b + jp + 1)
                        for t in range(TT):
                            mm = MM(y_bank(t // 2)[:, t % 2], HID[0:wd, jp % 3, t * P:(t + 1) * P],
                                    PROJ[0:wd, jp], start=jp == 0 and t % 2 == 0, stop=jp == FC - 1,
                                    skip_group_check=True)
                        mm.then_inc(y_part, 1)

            def project(b, q):
                for w in range(4):
                    weight, m = (WQ, WK)[w // 2], w % 2
                    need(pe, q_rest, 4 * b + w - 3)
                    for c in range(CT):
                        mm = MM(PS[:, 2 + w], weight[:, c, m * P:(m + 1) * P], XNT[:, q, c],
                                start=c == 0, stop=c == CT - 1)
                    mm.then_inc(q_mm, 1)
                for t in range(TT):
                    if t % 2 == 0:
                        need(pe, v_ready, 2 * b + t // 2 - 1)
                    for c in range(CT):
                        mm = MM(PS[:, t // 2, (t % 2) * C:(t % 2 + 1) * C], XNT[:, q, c, t * P:(t + 1) * P],
                                WV[:, c], start=c == 0, stop=c == CT - 1)
                    if t % 2:
                        mm.then_inc(v_mm, 1)

            def top_scores(b, q, k):
                h, t = divmod(k, TT)
                need(pe, top_ready, 64 * b + k - 1)
                MM(PS[:, k % 2], QS[q][0:KROWS, h, t * P:(t + 1) * P], KS[q][0:KROWS, h],
                   start=True, stop=True).then_inc(top_mm, 1)

            def neg_transpose(b, g):
                pe.wait_ge(neg_step, 16 * b + 4 * g + 4)
                for t in range(TT):
                    mm = nc.tensor.transpose(MISCB[0:3 * HG, t * P:(t + 1) * P],
                                             NP[:, g % 2, t].rearrange("p n h -> p (n h)"), IDENTB[:])
                mm.then_inc(neg_t, 1)

            def scores(b, q, g, kt):
                if kt == 0:
                    pe.wait_ge(nm_in[g], 16 * b + 16)
                for j in range(2):
                    need(pe, exp_done, 32 * b + 8 * g + 2 * kt + j - 1)
                    for k in range(2):
                        h = HG * g + 2 * j + k
                        mm = MM(PS[:, 2 + 2 * j + k], KS[q][0:MROWS, h, kt * P:(kt + 1) * P],
                                QS[q][0:MROWS, h], start=True, stop=True)
                    mm.then_inc(s_mm, 1)

            def weigh(b, q, g, kt):
                need(pe, exp_done, 32 * b + 8 * g + 2 * kt + 2)
                if kt == 0:
                    need(pe, u_ready, 4 * b + g)
                for k in range(HG):
                    mm = MM(PS[32 * k:32 * k + 32, 6], VA[:, q, kt, HG * g + k], PR[:, kt % 2, k],
                            start=kt == 0, stop=kt == TT - 1)
                mm.then_inc(pv_done, 1)

            def spread_sums(b, g):
                need(pe, u_ready, 4 * b + g + 1)
                MM(MISC, SUMSEL[:], U[:, g % 2], start=True, stop=True).then_inc(sum_mm, 1)

            def out_project(b):
                need(pe, o_ready, 4 * b + GR)
                for t in range(TT):
                    if t == 2:
                        need(pe, resid_c, 2 * b + 1)
                    for g in range(GR):
                        mm = MM(MISC[:, (t % 2) * C:(t % 2 + 1) * C], OT[:, g, t * P:(t + 1) * P], WO[:, g],
                                start=g == 0, stop=g == GR - 1)
                    if t % 2:
                        mm.then_inc(wo_mm, 1)

            pe.wait_ge(attn_in, 64)
            pe.wait_ge(k_ones, 2)
            need(pe, resid_b, 2 * B)
            with pe.Fori(0, PAIRS) as i:
                e, o = 2 * i, 2 * i + 1
                pe.wait_ge(xnt_ready, 2 * e + 18)
                need(pe, exp_done, 64 * i)
                need(pe, top_ready, 128 * i)
                project(e, 0)
                need(pe, resid_c, 2 * e)
                for c in range(CT):
                    ln_transpose(pe, 9 + e, 1, c)
                pe.wait_ge(xnt_ready, 2 * o + 18)
                project(o, 1)
                pe.wait_ge(stack_in[0], 16 * 24 * (i + 1))
                need(pe, v_ready, 4 * i + 4)
                for g in range(GR):
                    for k in range(16):
                        top_scores(e, 0, 16 * g + k)
                    if g:
                        if g > 1:
                            pe.wait_ge(nt_ready, 4 * e + g - 1)
                        neg_transpose(e, g - 1)
                pe.wait_ge(nt_ready, 4 * e + GR - 1)
                neg_transpose(e, GR - 1)
                pe.wait_ge(stack_in[1], 16 * 24 * (i + 1))
                need(pe, q_rest, 4 * o + 4)
                pe.wait_ge(nt_ready, 4 * e + GR)
                for s in range(4 * GR + 1):
                    g, kt = divmod(s, 4)
                    if s < 4 * GR:
                        for k in range(4):
                            top_scores(o, 1, 4 * s + k)
                        scores(e, 0, g, kt)
                    if s:
                        weigh(e, 0, (s - 1) // 4, (s - 1) % 4)
                    if kt == 1 and g:
                        if g > 1:
                            pe.wait_ge(nt_ready, 4 * o + g - 1)
                        spread_sums(e, g - 1)
                        pe.wait_ge(rc_ready, 4 * e + g)
                        neg_transpose(o, g - 1)
                pe.wait_ge(nt_ready, 4 * o + GR - 1)
                spread_sums(e, GR - 1)
                pe.wait_ge(rc_ready, 4 * e + GR)
                neg_transpose(o, GR - 1)
                pe.wait_ge(nt_ready, 4 * o + GR)
                out_project(e)
                need(pe, resid_c, 2 * e + 2)
                for c in range(CT):
                    ln_transpose(pe, 9 + o, 0, c)
                pe.wait_ge(xnt_ready, 2 * o + 20)
                for s in range(4 * GR + 1):
                    g, kt = divmod(s, 4)
                    if s < 4 * GR:
                        scores(o, 1, g, kt)
                    if s:
                        weigh(o, 1, (s - 1) // 4, (s - 1) % 4)
                    if kt == 1 and g:
                        if g > 1:
                            pe.wait_ge(rc_ready, 4 * o + g - 1)
                        spread_sums(o, g - 1)
                pe.wait_ge(rc_ready, 4 * o + GR - 1)
                spread_sums(o, GR - 1)
                pe.wait_ge(rc_ready, 4 * o + GR)
                out_project(o)

            need(pe, resid_c, 2 * B)
            for b, p in batches(pe):
                pe.wait_ge(x_part3, b + 1)
                moving = [XNT[:, p].bitcast(bf16)[:, :, 1:2 * T:2], XR[:, p].bitcast(bf16)[:, :, 1:2 * T:2],
                          X3[:, p]]
                for j in range(DC + 2):
                    if j < DC:
                        need(pe, ge_ready, DC * b + j - 1)
                        for c in range(CT):
                            for n in range(3):
                                mm = MM(PS[:, j % 2], W1Q[:, c, j * P:(j + 1) * P], moving[n][:, c],
                                        start=c + n == 0, stop=c == CT - 1 and n == 2)
                        mm.then_inc(ff_mm, 1)
                    if j in (5, 6):
                        ln_transpose(pe, 13 + b, 1 - p, j - 5)
                    jp = j - 2
                    if jp >= 0:
                        if jp == 0:
                            need(pe, resid_d, 2 * b)
                        pe.wait_ge(g_part3, DC * b + jp + 1)
                        left = [GE[:, jp % 3].bitcast(bf16)[:, 1:2 * T:2], GREM[:, jp % 3].bitcast(bf16)[:, 1:2 * T:2],
                                G3[:, jp % 3]]
                        for t in range(TT):
                            for n in range(3):
                                mm = MM(y_bank(t // 2)[:, t % 2], left[n][:, t * P:(t + 1) * P], W2Q[:, jp],
                                        start=jp + n == 0 and t % 2 == 0, stop=jp == DC - 1 and n == 2,
                                        skip_group_check=True)
                        mm.then_inc(yf_part, 1)


_OUT = (B, T, C)


def kernel(L0_attn_x, L0_attn_W, L0_attn_b, L0_ffn_gate_w, L0_ffn_expert_fc1, L0_ffn_expert_fc2,
           L0_ffn_expert_proj, L0_ffn_shared_fc1, L0_ffn_shared_fc2, L0_ffn_shared_proj,
           L0_ffn_shared_gate_w, L1_attn_Wq, L1_attn_Wk, L1_attn_Wv, L1_attn_Wo, L1_ffn_w1, L1_ffn_b1,
           L1_ffn_w2, L1_ffn_b2):
    import ml_dtypes
    import numpy as np
    import concourse.bacc as bacc
    from concourse.bass_utils import run_bass_kernel_spmd

    def a(v):
        return np.asarray(v)

    def rows(w):
        wt = a(w).T
        return np.ascontiguousarray(wt.reshape(-1, P, wt.shape[1]).transpose(1, 0, 2))

    fc1 = np.concatenate([a(L0_ffn_expert_fc1).reshape(NE * FE, C), a(L0_ffn_shared_fc1)])
    fc2 = np.concatenate([a(L0_ffn_expert_fc2).reshape(NE * FE, C), a(L0_ffn_shared_fc2)])
    pj = np.concatenate([a(L0_ffn_expert_proj).transpose(0, 2, 1).reshape(NE * FE, C),
                         a(L0_ffn_shared_proj).T])
    pj = np.concatenate([pj, np.zeros((FC * P - F, C), pj.dtype)])
    wo = np.zeros((GR, HG, 32, C), np.float32)
    wo[:, :, :HD] = a(L1_attn_Wo).T.reshape(GR, HG, HD, C)
    expert_of = np.minimum(np.arange(F) // FE, NE)
    k = np.arange(P)
    sumsel = (k[:, None] % 32 == HD) & (k[:, None] // 32 == k[None, :] // 32)
    low = np.arange(NE)[None, :] < np.arange(NE)[:, None]
    data = {
        "x": a(L0_attn_x),
        "w0": rows(L0_attn_W),
        "b0": np.ascontiguousarray(a(L0_attn_b).reshape(4, P).T),
        "fc1": rows(fc1), "fc2": rows(fc2),
        "proj": np.ascontiguousarray(pj.reshape(FC, P, C).transpose(1, 0, 2)),
        "gate": rows(np.concatenate([a(L0_ffn_gate_w), a(L0_ffn_shared_gate_w)])),
        "sel": np.tile(np.arange(NG)[:, None] == expert_of[None, :], (3, 1)).astype(ml_dtypes.bfloat16),
        "wq": rows(L1_attn_Wq), "wk": rows(L1_attn_Wk), "wv": rows(L1_attn_Wv),
        "wo": np.ascontiguousarray(wo.reshape(GR, P, C).transpose(1, 0, 2)),
        "w1": rows(L1_ffn_w1),
        "b1": np.ascontiguousarray(a(L1_ffn_b1).reshape(DC, P).T),
        "w2": rows(L1_ffn_w2),
        "b2": np.ascontiguousarray(np.broadcast_to(a(L1_ffn_b2), (P, C))),
        "ident": np.eye(P, dtype=np.float32),
        "identb": np.eye(P, dtype=np.float32).astype(ml_dtypes.bfloat16),
        "sumsel": sumsel.astype(np.float32),
        "lower": np.ascontiguousarray(np.broadcast_to(low, (P, NE, NE))).astype(np.float32),
    }
    nc = bacc.Bacc("TRN2", target_bir_lowering=False, num_devices=1)
    arrays, args = {}, {}
    for name, v in data.items():
        arrays[f"in_{name}"] = v
        args[name] = nc.dram_tensor(f"in_{name}", v.shape, mybir.dt.from_np(v.dtype), kind="ExternalInput").ap()
    args["out"] = nc.dram_tensor("out_0", _OUT, mybir.dt.float32, kind="ExternalOutput").ap()
    build(nc, **args)
    r = run_bass_kernel_spmd(nc, [arrays], core_ids=[0])
    return r.results[0]["out_0"]
```

```python
import concourse.bass as bass
from concourse import mybir
from contextlib import ExitStack

B, T, C = 4, 512, 256
P = 128
CT = C // P
TT = T // P
NE, TOPK = 8, 2
FE, FS = 176, 704
F = NE * FE + FS
FC = -(-F // P)
NG = NE + 1
H, HD = 16, 16
HG = 4
GR = H // HG
DFF = 1024
DC = DFF // P
EPS = 1e-5
PAIRS = B // 2
LAG = 4
QPART, KPART = (0, 0, 1, 1, 0, 2), (0, 1, 0, 1, 2, 0)
KROWS = HD * len(QPART)
MROWS = KROWS + 3
QK_ORDER = (0, 2, 1, 3)
STEPS = GR * TT
LN_STEPS, OUT_STEPS, NEG_STEPS, QK_STEPS = (3, 4), (5, 9, 13), (6, 10, 14), (7, 8, 11, 12)


def width(j):
    return min(P, F - j * P)


def build(nc, x, w0, b0, fc1, fc2, proj, gate, sel, wq, wk, wv, wo, w1, b1, w2, b2,
          ident, identb, kones, lower, out):
    f32, bf16 = mybir.dt.float32, mybir.dt.bfloat16
    ALU, ACT, AX = mybir.AluOpType, mybir.ActivationFunctionType, mybir.AxisListType

    ctx = ExitStack()
    with ctx:
        def sb(name, shape, dt):
            return ctx.enter_context(nc.sbuf_tensor(name, shape, dt))

        def sem(name):
            return ctx.enter_context(nc.semaphore(name))

        X = sb("X", [P, B * TT, C], f32)
        XN = sb("XN", [P, 2, TT, C], f32)
        XNT = sb("XNT", [P, 2, CT, T], f32)
        STATS = sb("STATS", [P, 2, TT, 6], f32)
        MV = sb("MV", [P, 2, TT, 2], f32)
        VE = sb("VE", [P, 2, TT], f32)
        RSTD = sb("RSTD", [P, 2, TT], f32)
        MHALF = sb("MHALF", [P, TT], f32)
        IDENT = sb("IDENT", [P, P], f32)
        IDENTB = sb("IDENTB", [P, P], bf16)
        LOWER = sb("LOWER", [P, NE, NE], f32)
        ONES = sb("ONES", [P, P], f32)
        SEL = sb("SEL", [3 * NG, F], bf16)
        B0 = sb("B0", [P, 4], f32)
        GATE = sb("GATE", [P, CT, NG], f32)
        WQ = sb("WQ", [P, CT, C], f32)
        WK = sb("WK", [P, CT, C], f32)
        WV = sb("WV", [P, CT, C], f32)
        WO = sb("WO", [P, CT, C], f32)
        B1 = sb("B1", [P, DC], f32)
        B2 = sb("B2", [1, C], f32)
        W1Q = sb("W1Q", [P, CT, DFF], bf16)
        W2Q = sb("W2Q", [P, DC, C], bf16)

        BIG = sb("BIG", [P, 4 * H * T // 2], f32)
        FC1 = BIG[:, 0:CT * F].rearrange("p (k f) -> p k f", k=CT)
        FC2 = BIG[:, CT * F:2 * CT * F].rearrange("p (k f) -> p k f", k=CT)
        PROJ = BIG[:, 2 * CT * F:2 * CT * F + FC * C].rearrange("p (j c) -> p j c", j=FC)
        STACK = BIG[:].bitcast(bf16).rearrange("p (s h t) -> p s h t", s=4, h=H)
        QS = [STACK[:, p] for p in range(2)]
        KS = [STACK[:, 2 + p] for p in range(2)]

        WORKA = sb("WORKA", [P, 12 * T], f32)
        GV = WORKA[:, 0:8 * T].rearrange("p (b m t) -> p b m t", b=2, m=4)
        HS = WORKA[:, 8 * T:12 * T].rearrange("p (b m t) -> p b m t", b=2, m=CT)
        SILU = WORKA[:, 0:2 * T].rearrange("p (r t) -> p r t", r=2)
        UP = WORKA[:, 2 * T:8 * T].rearrange("p (r t) -> p r t", r=6)
        HID = WORKA[:, 8 * T:11 * T].rearrange("p (r t) -> p r t", r=3)
        PR = WORKA[:, 0:8 * T].rearrange("p (r h t) -> p r h t", r=2, h=HG)
        WORKB = sb("WORKB", [P, 8 * T], f32)
        RAW1 = WORKB[:, 0:4 * T].rearrange("p (k f) -> p k f", k=CT)
        RAW2 = WORKB[:, 4 * T:8 * T].rearrange("p (k f) -> p k f", k=DC)
        VA = WORKB[:, :].rearrange("p (b t h d) -> p b t h d", b=2, t=TT, h=H)
        WORKC = sb("WORKC", [P, 16 * T], f32)
        W0 = WORKC[:, 14 * T:16 * T].rearrange("p (k f) -> p k f", k=CT)
        QP = WORKC[:, 0:6 * T].bitcast(bf16).rearrange("p (w n t) -> p w n t", w=4, n=3)
        REST = WORKC[:, 6 * T:8 * T].rearrange("p (r t) -> p r t", r=2)
        U = WORKC[:, 8 * T:10 * T].rearrange("p (r t) -> p r t", r=2)
        OTOK = WORKC[:, 10 * T:12 * T].rearrange("p (t h d) -> p t h d", t=TT, h=H)
        OT = WORKC[:, 12 * T:14 * T].rearrange("p (c t) -> p c t", c=CT)
        NT = WORKC[:, 15 * T:16 * T].bitcast(bf16).rearrange("p (r t) -> p r t", r=2)
        QTMP = [WORKC[:, 4 * T * k:4 * T * (k + 1)] for k in range(2)]
        XR = WORKC[:, 0:4 * T].rearrange("p (b k t) -> p b k t", b=2, k=CT)
        X3 = WORKC[:, 4 * T:6 * T].bitcast(bf16).rearrange("p (b k t) -> p b k t", b=2, k=CT)
        GE = WORKC[:, 6 * T:9 * T].rearrange("p (r t) -> p r t", r=3)
        GREM = WORKC[:, 9 * T:12 * T].rearrange("p (r t) -> p r t", r=3)
        G3 = WORKC[:, 12 * T:12 * T + 3 * T // 2].bitcast(bf16).rearrange("p (r t) -> p r t", r=3)

        LOGIT = sb("LOGIT", [NG, T], f32)
        ROWMAX = sb("ROWMAX", [P, TT], f32)
        ZE = sb("ZE", [P, TT, NE], f32)
        ZS = sb("ZS", [P, TT], f32)
        EE = sb("EE", [P, TT, NE], f32)
        ES = sb("ES", [P, TT], f32)
        ESUM = sb("ESUM", [P, TT], f32)
        ERCP = sb("ERCP", [P, TT], f32)
        GT = sb("GT", [P, TT, NE, NE], f32)
        EQ = sb("EQ", [P, TT, NE, NE], f32)
        RANK = sb("RANK", [P, TT, NE], f32)
        SELE = sb("SELE", [P, TT, NE], f32)
        COMB = sb("COMB", [P, TT, NG], f32)
        CREM = sb("CREM", [P, TT, NG], f32)
        CPART = sb("CPART", [P, TT, 3, NG], bf16)
        COMBT = sb("COMBT", [3 * NG, 2, T], bf16)
        MX = sb("MX", [P, 2, H, TT], f32)
        RECIP = sb("RECIP", [P, 2, TT, HG], f32)
        NREM = sb("NREM", [P, HG, TT], f32)
        NP = sb("NP", [P, 2, TT, 3, HG], bf16)
        WSUM = sb("WSUM", [P, 2], f32)
        WMEAN = sb("WMEAN", [P, 2], f32)
        THR = sb("THR", [P, 2], f32)
        NTHR = sb("NTHR", [P, 2], f32)

        PS = ctx.enter_context(nc.psum_tensor("PS", [P, 8, 512], f32))
        MISC = PS[:, 7]
        MISCB = MISC.bitcast(bf16)

        qk_dram = nc.dram_tensor("qk_parts", [B, 4, 3, P, T], bf16, kind="Internal").ap()
        nm_dram = nc.dram_tensor("neg_max_parts", [B, GR, 3 * HG, T], bf16, kind="Internal").ap()

        held = sem("held")
        x_first, x_rest = sem("x_first"), sem("x_rest")
        w0_in, ident_in, const_in, mix_in, attn_in, ffn_in = (sem(n) for n in (
            "w0_in", "ident_in", "const_in", "mix_in", "attn_in", "ffn_in"))
        ones_set, half_set = sem("ones_set"), sem("half_set")
        ln_stats, ln_mv, ln_var, ln_rstd, xn_ready, xnt_psum, xnt_ready = (sem(n) for n in (
            "ln_stats", "ln_mv", "ln_var", "ln_rstd", "xn_ready", "xnt_psum", "xnt_ready"))
        scan_mm, scan_act, scanned, back_mm, resid_a = (sem(n) for n in (
            "scan_mm", "scan_act", "scanned", "back_mm", "resid_a"))
        (logit_mm, logit_sb, logit_t, router_step, comb_step, router_z, router_e, comb_mm, comb_ready,
         h1_mm, h2_mm, silu_ready, up_ready, c_mm, hid_ready, y_part, resid_b) = (sem(n) for n in (
            "logit_mm", "logit_sb", "logit_t", "router_step", "comb_step", "router_z", "router_e", "comb_mm",
            "comb_ready", "h1_mm", "h2_mm", "silu_ready", "up_ready", "c_mm", "hid_ready",
            "y_part", "resid_b"))
        wabs, wtot, wstep, tern_ready = (sem(n) for n in ("wabs", "wtot", "wstep", "tern_ready"))
        above = sem("above")
        (q_mm, q_part1, q_rest, q_part2, q_part3, v_mm, v_ready, k_ones, v_ones, top_mm, top_ready,
         neg_step, neg_t, nt_ready, s_mm, exp_done, pv_done, u_ready, ut_mm, recip_ready, otok_ready,
         ob_mm, o_ready, wo_mm, resid_c) = (sem(n) for n in (
            "q_mm", "q_part1", "q_rest", "q_part2", "q_part3", "v_mm", "v_ready", "k_ones", "v_ones",
            "top_mm", "top_ready", "neg_step", "neg_t", "nt_ready", "s_mm", "exp_done", "pv_done",
            "u_ready", "ut_mm", "recip_ready", "otok_ready", "ob_mm", "o_ready", "wo_mm", "resid_c"))
        parts_out = [sem(f"parts_out{w}") for w in range(4)]
        stack_in = [[sem(f"stack_in{p}{half}") for half in range(2)] for p in range(2)]
        nm_out = [sem(f"nm_out{g}") for g in range(GR)]
        nm_in = [sem(f"nm_in{g}") for g in range(GR)]
        (x_rem, x_part3, ff_mm, ge_ready, g_rem, g_part3, yf_part, resid_d, stored) = (
            sem(n) for n in ("x_rem", "x_part3", "ff_mm", "ge_ready", "g_rem", "g_part3", "yf_part",
                             "resid_d", "stored"))

        CREDIT = {scan_act: 4, resid_a: 2, silu_ready: 2, up_ready: 2, hid_ready: 1, y_part: 3,
                  resid_b: 2, q_rest: 4, q_part3: 2, top_ready: 2, exp_done: 2, pv_done: 2, v_ready: 2,
                  u_ready: 1, resid_c: 2, ge_ready: 2, yf_part: 3, resid_d: 2}
        for w in range(4):
            CREDIT[parts_out[w]] = 16
            CREDIT[nm_out[w]] = 16

        def need(eng, s, n):
            eng.wait_ge(s, n + CREDIT.get(s, 0))

        def hold(eng, s, n):
            need(eng, s, n)
            eng.sem_inc(held, 1)

        def batches(eng):
            with eng.Fori(0, PAIRS) as i:
                for p in range(2):
                    yield 2 * i + p, p

        def following(b, p):
            return b + 1 if p == 0 else B - 1 - b

        def attention_batches(eng):
            with eng.Fori(0, PAIRS - 1) as i:
                for p in range(2):
                    yield 2 * i + p, p, i, 2
            for p in range(2):
                yield B - 2 + p, p, PAIRS - 1, 1 - p

        def tiles(b, j=0, n=TT):
            return bass.ds(TT * b + j, n)

        def y_bank(j):
            return PS[:, 5 + j].rearrange("p (t c) -> p t c", t=2)

        def ln_stats_of(dve, n, q, src):
            for t in range(TT):
                nc.vector.bn_stats(STATS[:, q, t], X[:, bass.ds(src * TT + t, 1)]).then_inc(ln_stats, 1)
            hold(dve, ln_stats, 4 * n + 4)
            for t in range(TT):
                nc.vector.bn_aggr(MV[:, q, t], STATS[:, q, t]).then_inc(ln_mv, 1)

        def ln_rstd_of(pool, n, q):
            hold(pool, ln_mv, 4 * n + 4)
            nc.gpsimd.tensor_scalar(VE[:, q], MV[:, q, :, 1], EPS, None, ALU.add).then_inc(ln_var, 1)
            pool.wait_ge(ln_var, n + 1)
            nc.gpsimd.tensor_tensor(RSTD[:, q], VE[:, q], MHALF[:], ALU.pow).then_inc(ln_rstd, 1)

        def ln_scale(dve, n, q, src):
            hold(dve, ln_rstd, n + 1)
            for t in range(TT):
                nc.vector.tensor_scalar(XN[:, q, t], X[:, bass.ds(src * TT + t, 1)].rearrange("p a c -> p (a c)"),
                                        MV[:, q, t, 0:1], RSTD[:, q, t:t + 1],
                                        ALU.subtract, ALU.mult).then_inc(xn_ready, 1)

        def ln_transpose(pe, n, q, c):
            pe.wait_ge(xn_ready, TT * n + TT)
            if c == 1:
                pe.wait_ge(xnt_ready, 2 * n + 1)
            for t in range(TT):
                mm = nc.tensor.transpose(MISC[:, t * P:(t + 1) * P], XN[:, q, t, c * P:(c + 1) * P], IDENT[:])
            mm.then_inc(xnt_psum, 1)

        def ln_copy(act, n, q, c):
            act.wait_ge(xnt_psum, 2 * n + c + 1)
            nc.scalar.activation(XNT[:, q, c], MISC, ACT.Copy).then_inc(xnt_ready, 1)

        block = ctx.enter_context(nc.Block())

        @block.sync
        def _(sp):
            for s, n in CREDIT.items():
                sp.sem_inc(s, n)
            xt = x.rearrange("b (t p) c -> b p t c", p=P)
            sp.dma_start(X[:, 0:TT], xt[0]).then_inc(x_first, 16)
            sp.dma_start(IDENT[:], ident).then_inc(ident_in, 16)
            sp.dma_start(W0, w0).then_inc(w0_in, 16)
            sp.dma_start(B0[:], b0).then_inc(w0_in, 16)
            for b in range(1, B):
                sp.dma_start(X[:, b * TT:(b + 1) * TT], xt[b]).then_inc(x_rest, 16)
            for dst, src in ((RAW1, w1), (RAW2, w2), (B1[:], b1), (B2[:], b2)):
                sp.dma_start(dst, src).then_inc(ffn_in, 16)
            for dst, src in ((IDENTB, identb), (LOWER, lower), (SEL, sel)):
                sp.dma_start(dst[:], src).then_inc(const_in, 16)
            for dst, src in ((GATE[:], gate), (FC1, fc1), (FC2, fc2), (PROJ, proj)):
                sp.dma_start(dst, src).then_inc(mix_in, 16)
            for dst, src in ((WQ, wq), (WK, wk), (WV, wv), (WO, wo)):
                sp.dma_start(dst[:], src).then_inc(attn_in, 16)

            def parts(b, k):
                w = QK_ORDER[k]
                need(sp, q_part3, 4 * b + k + 1)
                sp.dma_start(qk_dram[bass.ds(b, 1), w].rearrange("a n p t -> p (a n) t"),
                             QP[:, w]).then_inc(parts_out[w], 16)

            def stack(b, q, half):
                for w, part, dst in ((half, QPART, QS[q]), (2 + half, KPART, KS[q])):
                    need(sp, parts_out[w], 16 * b + 16)
                    h0 = half * (H // 2)
                    for g, n in enumerate(part):
                        sp.dma_start(dst[HD * g:HD * (g + 1), h0:h0 + H // 2],
                                     qk_dram[bass.ds(b, 1), w, n].rearrange("a (h d) t -> d (a h) t", d=HD)
                                     ).then_inc(stack_in[q][half], 16)

            def neg_rows(b, g, q):
                sp.wait_ge(nt_ready, 4 * b + g + 1)
                sp.dma_start(nm_dram[bass.ds(b, 1), g].rearrange("a r t -> (a r) t"),
                             NT[0:3 * HG, g % 2]).then_inc(nm_out[g], 16)
                need(sp, nm_out[g], 16 * b + 16)
                sp.dma_start(QS[q][KROWS:MROWS, HG * g:HG * (g + 1)],
                             nm_dram[bass.ds(b, 1), g].rearrange("a (n h) t -> (a n) h t", n=3)
                             ).then_inc(nm_in[g], 16)

            need(sp, resid_b, 2 * B)
            for q in range(2):
                sp.dma_start(KS[q][KROWS:MROWS], kones).then_inc(k_ones, 16)
            for b in range(2):
                for k in range(4):
                    parts(b, k)
                    if k % 2:
                        stack(b, b, k // 2)
            for g in range(GR):
                neg_rows(0, g, 0)
            for b, p, i, left in attention_batches(sp):
                for g in range(GR):
                    if left == 2 and g == GR - 1:
                        need(sp, s_mm, 32 * b + 32)
                        stack(b + 2, p, 1)
                    if left:
                        neg_rows(b + 1, g, 1 - p)
                    if left == 2 and g < 2:
                        parts(b + 2, 2 * g)
                        parts(b + 2, 2 * g + 1)
                        if g == 0:
                            need(sp, s_mm, 32 * b + 16)
                            stack(b + 2, p, 0)
            ot = out.rearrange("b (t p) c -> b p t c", p=P)
            with sp.Fori(0, B) as b:
                need(sp, resid_d, 2 * b + 2)
                sp.dma_start(ot[bass.ds(b, 1)].rearrange("a p t c -> p (a t) c"),
                             X[:, tiles(b)]).then_inc(stored, 16)
            sp.wait_ge(stored, 16 * B)

        @block.gpsimd
        def _(pool):
            nc.gpsimd.memset(MHALF[:], -0.5).then_inc(half_set, 1)
            nc.gpsimd.memset(ONES[:], 1.0).then_inc(ones_set, 1)
            pool.wait_ge(half_set, 1)
            ln_rstd_of(pool, 0, 0)
            for b, p in batches(pool):
                ln_rstd_of(pool, b + 1, 1 - p)
            hold(pool, wstep, 3)
            for k, (raw, tern) in enumerate(((RAW1, W1Q), (RAW2, W2Q))):
                raw, tern = raw.rearrange("p k f -> p (k f)"), tern[:].rearrange("p k f -> p (k f)")
                if k:
                    hold(pool, tern_ready, k)
                nc.gpsimd.tensor_scalar(QTMP[0], raw, THR[:, k:k + 1], None, ALU.is_ge).then_inc(above, 1)
                nc.gpsimd.tensor_scalar(QTMP[1], raw, NTHR[:, k:k + 1], None, ALU.is_le).then_inc(above, 1)
                pool.wait_ge(above, 2 * k + 2)
                nc.gpsimd.tensor_tensor(tern, QTMP[0], QTMP[1], ALU.subtract).then_inc(tern_ready, 1)
            pool.wait_ge(tern_ready, 2)
            for p in range(2):
                nc.gpsimd.memset(VA[:, p, :, :, HD:2 * HD], 1.0).then_inc(v_ones, 1)
            for b, p in batches(pool):
                ln_rstd_of(pool, b + 5, 1 - p)
            def part3(b, k):
                w = QK_ORDER[k]
                pool.wait_ge(q_part2, 4 * b + k + 1)
                nc.gpsimd.tensor_tensor(QP[:, w, 2], REST[:, k % 2], QP[:, w, 1],
                                        ALU.subtract).then_inc(q_part3, 1)

            ln_rstd_of(pool, 9, 1)
            for b in range(2):
                for k in range(4):
                    part3(b, k)
            for b, p, i, left in attention_batches(pool):
                if left:
                    ln_rstd_of(pool, b + 10, p)
                if left == 2:
                    for k in range(4):
                        part3(b + 2, k)
            for b, p in batches(pool):
                ln_rstd_of(pool, 13 + b, 1 - p)
                for j in range(DC):
                    pool.wait_ge(g_rem, DC * b + j + 1)
                    need(pool, yf_part, DC * b + j - 2)
                    nc.gpsimd.tensor_tensor(G3[:, j % 3], GREM[:, j % 3],
                                            GREM[:, j % 3].bitcast(bf16)[:, 1:2 * T:2],
                                            ALU.subtract).then_inc(g_part3, 1)

        @block.scalar
        def _(act):
            for c in range(CT):
                ln_copy(act, 0, 0, c)
            act.wait_ge(w0_in, 32)
            for b, p in batches(act):
                for k, m in enumerate((0, 2, 1, 3)):
                    act.wait_ge(scan_mm, 4 * b + k + 1)
                    nc.scalar.activation(GV[:, p, m], PS[:, m], ACT.Sigmoid if m < 2 else ACT.Tanh,
                                         bias=B0[:, m:m + 1]).then_inc(scan_act, 1)
                for c in range(CT):
                    ln_copy(act, b + 1, 1 - p, c)
            act.wait_ge(ffn_in, 64)
            nc.scalar.activation(QTMP[0], RAW1.rearrange("p k f -> p (k f)"), ACT.Abs,
                                 accum_out=WSUM[:, 0:1]).then_inc(wabs, 1)
            nc.scalar.activation(QTMP[1], RAW2.rearrange("p k f -> p (k f)"), ACT.Abs,
                                 accum_out=WSUM[:, 1:2]).then_inc(wabs, 1)
            for b, p in batches(act):
                act.wait_ge(logit_mm, b + 1)
                nc.scalar.activation(LOGIT[:], MISC[0:NG], ACT.Copy).then_inc(logit_sb, 1)
                for j in range(FC):
                    act.wait_ge(h1_mm, FC * b + j + 1)
                    need(act, up_ready, FC * b + j - 1)
                    nc.scalar.activation(SILU[0:width(j), j % 2], PS[0:width(j), j % 2],
                                         ACT.Silu).then_inc(silu_ready, 1)
                    if j == 0:
                        act.wait_ge(router_z, 2 * b + 2)
                        nc.scalar.activation(EE[:], ZE[:], ACT.Exp).then_inc(router_e, 1)
                        nc.scalar.activation(ES[:], ZS[:], ACT.Exp, scale=-1.0).then_inc(router_e, 1)
                    if j == 3:
                        act.wait_ge(comb_mm, b + 1)
                        nc.scalar.activation(COMBT[:, p], MISCB[0:3 * NG, 0:T], ACT.Copy).then_inc(comb_ready, 1)
                    if j in (8, 9):
                        ln_copy(act, 5 + b, 1 - p, j - 8)

            def part1(b, k, bank):
                w = QK_ORDER[k]
                act.wait_ge(q_mm, 4 * b + k + 1)
                need(act, parts_out[w], 16 * b)
                nc.scalar.activation(QP[:, w, 0], PS[:, bank], ACT.Copy).then_inc(q_part1, 1)

            def part2(b, k):
                need(act, q_rest, 4 * b + k + 1)
                nc.scalar.activation(QP[:, QK_ORDER[k], 1], REST[:, k % 2], ACT.Copy).then_inc(q_part2, 1)

            def v_copy(b, q, j):
                act.wait_ge(v_mm, 2 * b + j + 1)
                nc.scalar.activation(VA[:, q, 2 * j:2 * j + 2, :, 0:HD],
                                     PS[:, j].rearrange("p (t h d) -> p t h d", t=2, h=H),
                                     ACT.Copy).then_inc(v_ready, 1)

            def nt_copy(b, g):
                act.wait_ge(neg_t, 4 * b + g + 1)
                need(act, nm_out[(g + 2) % GR], 16 * b + 16 * (g // 2))
                nc.scalar.activation(NT[0:3 * HG, g % 2], MISCB[0:3 * HG, 0:T], ACT.Copy).then_inc(nt_ready, 1)

            def exps(b, s, j):
                act.wait_ge(s_mm, 32 * b + 2 * s + j + 1)
                if j == 0:
                    need(act, pv_done, 16 * b + s - 1)
                nc.scalar.activation(PR[:, s % 2, 2 * j:2 * j + 2],
                                     PS[:, 2 + 2 * j:4 + 2 * j], ACT.Exp, scale=0.25).then_inc(exp_done, 1)

            def u_copy(b, g):
                need(act, pv_done, 16 * b + 4 * g + 4)
                nc.scalar.activation(U[:, g % 2], PS[:, 6], ACT.Copy).then_inc(u_ready, 1)

            act.wait_ge(v_ones, 2)
            for b in range(2):
                for k in range(4):
                    part1(b, k, 2 + k)
                    if k:
                        part2(b, k - 1)
                part2(b, 3)
                for j in range(2):
                    v_copy(b, b, j)
                if b == 0:
                    for c in range(CT):
                        ln_copy(act, 9, 1, c)
            for g in range(GR):
                nt_copy(0, g)
            for b, p, i, left in attention_batches(act):
                for s in range(STEPS):
                    exps(b, s, 0)
                    if left and s in LN_STEPS:
                        ln_copy(act, b + 10, p, LN_STEPS.index(s))
                    if left and s in NEG_STEPS:
                        nt_copy(b + 1, NEG_STEPS.index(s))
                    if left == 2 and s in QK_STEPS:
                        part1(b + 2, QK_STEPS.index(s), 7)
                    if left == 2 and s - 1 in QK_STEPS:
                        part2(b + 2, QK_STEPS.index(s - 1))
                    exps(b, s, 1)
                    if s + 1 in OUT_STEPS:
                        u_copy(b, OUT_STEPS.index(s + 1))
                u_copy(b, GR - 1)
                if left == 2:
                    for j in range(2):
                        v_copy(b + 2, p, j)
                if left:
                    nt_copy(b + 1, GR - 1)
                act.wait_ge(ob_mm, 2 * b + 1)
                nc.scalar.activation(OT[:, 0], PS[:, 2], ACT.Copy).then_inc(o_ready, 1)
            for b, p in batches(act):
                for j in range(DC):
                    act.wait_ge(ff_mm, DC * b + j + 1)
                    need(act, yf_part, DC * b + j - 2)
                    nc.scalar.activation(GE[:, j % 3], PS[:, j % 2], ACT.Gelu,
                                         bias=B1[:, j:j + 1]).then_inc(ge_ready, 1)
                    if j in (5, 6):
                        ln_copy(act, 13 + b, 1 - p, j - 5)

        @block.vector
        def _(dve):
            dve.wait_ge(x_first, 16)
            ln_stats_of(dve, 0, 0, 0)
            ln_scale(dve, 0, 0, 0)
            dve.wait_ge(x_rest, 16 * (B - 1))
            for b, p in batches(dve):
                hold(dve, resid_a, 2 * b)
                ln_stats_of(dve, b + 1, 1 - p, following(b, p))
                for c in range(CT):
                    if c:
                        ln_scale(dve, b + 1, 1 - p, following(b, p))
                    need(dve, scan_act, 4 * b + 2 * c + 2)
                    nc.vector.tensor_tensor_scan(HS[:, p, c], GV[:, p, c], GV[:, p, 2 + c], 0.0,
                                                 ALU.mult, ALU.add).then_inc(scanned, 1)
                for j in range(2):
                    dve.wait_ge(back_mm, 2 * b + j + 1)
                    xs = X[:, tiles(b, 2 * j, 2)]
                    nc.vector.tensor_tensor(xs, PS[:, 4 + j].rearrange("p (t c) -> p t c", t=2), xs,
                                            ALU.add).then_inc(resid_a, 1)
            dve.wait_ge(wtot, 1)
            nc.vector.tensor_scalar(WMEAN[:], MISC[:, 0:2], 1.0 / (C * DFF), None, ALU.mult).then_inc(wstep, 1)
            dve.wait_ge(wstep, 1)
            nc.vector.tensor_scalar(THR[:], WMEAN[:], 0.7, None, ALU.mult).then_inc(wstep, 1)
            dve.wait_ge(wstep, 2)
            nc.vector.tensor_scalar(NTHR[:], THR[:], -1.0, None, ALU.mult).then_inc(wstep, 1)
            RS = 13

            def router(b, k0, ops):
                for k, op in enumerate(ops, k0):
                    if k:
                        dve.wait_ge(router_step, RS * b + k)
                    op().then_inc(router_step, 1)

            V = nc.vector

            def bc_i(a):
                return a.unsqueeze(2).broadcast_to([P, TT, NE, NE])

            def bc_j(a):
                return a.unsqueeze(3).broadcast_to([P, TT, NE, NE])

            def bc_e(a, n=NE):
                return a.unsqueeze(2).broadcast_to([P, TT, n])

            LG = MISC[:, 0:16 * TT].rearrange("p (t e) -> p t e", t=TT)
            for b, p in batches(dve):
                hold(dve, resid_b, 2 * b)
                for j in range(FC + LAG):
                    if j < FC:
                        wd = width(j)
                        need(dve, silu_ready, FC * b + j + 1)
                        dve.wait_ge(h2_mm, FC * b + j + 1)
                        V.tensor_tensor(UP[0:wd, j % 6], PS[0:wd, 2 + j % 2], SILU[0:wd, j % 2],
                                        ALU.mult).then_inc(up_ready, 1)
                    if j == 0:
                        dve.wait_ge(logit_t, b + 1)
                        router(b, 0, [lambda: V.tensor_reduce(ROWMAX[:], LG[:, :, 0:NE], AX.X, ALU.max)])
                        dve.wait_ge(router_step, RS * b + 1)
                        V.tensor_tensor(ZE[:], LG[:, :, 0:NE], bc_e(ROWMAX[:]), ALU.subtract).then_inc(router_z, 1)
                        V.tensor_copy(ZS[:], LG[:, :, NE]).then_inc(router_z, 1)
                    if j == 1:
                        dve.wait_ge(router_e, 2 * b + 2)
                        router(b, 1, [
                            lambda: V.tensor_reduce(ESUM[:], EE[:], AX.X, ALU.add),
                            lambda: V.reciprocal(ERCP[:], ESUM[:]),
                            lambda: V.tensor_tensor(GT[:], bc_i(EE[:]), bc_j(EE[:]), ALU.is_gt),
                            lambda: V.tensor_tensor(EQ[:], bc_i(EE[:]), bc_j(EE[:]), ALU.is_equal),
                            lambda: V.tensor_tensor(EQ[:], EQ[:], LOWER[:].unsqueeze(1).broadcast_to(
                                [P, TT, NE, NE]), ALU.mult),
                            lambda: V.tensor_tensor(GT[:], GT[:], EQ[:], ALU.add),
                            lambda: V.tensor_reduce(RANK[:], GT[:], AX.X, ALU.add),
                            lambda: V.scalar_tensor_tensor(SELE[:], RANK[:], TOPK - 0.5, EE[:],
                                                           ALU.is_lt, ALU.mult),
                            lambda: V.tensor_tensor(COMB[:, :, 0:NE], SELE[:], bc_e(ERCP[:]), ALU.mult),
                            lambda: V.tensor_scalar(ESUM[:], ES[:], 1.0, None, ALU.add),
                            lambda: V.reciprocal(COMB[:, :, NE], ESUM[:]),
                            lambda: V.tensor_copy(CPART[:, :, 0], COMB[:]),
                        ])
                        assert RS == 13
                        dve.wait_ge(router_step, RS * b + RS)
                        V.tensor_tensor(CREM[:], COMB[:], CPART[:, :, 0], ALU.subtract).then_inc(comb_step, 1)
                        dve.wait_ge(comb_step, 3 * b + 1)
                        V.tensor_copy(CPART[:, :, 1], CREM[:]).then_inc(comb_step, 1)
                        dve.wait_ge(comb_step, 3 * b + 2)
                        V.tensor_tensor(CPART[:, :, 2], CREM[:], CPART[:, :, 1], ALU.subtract).then_inc(comb_step, 1)
                    if j == 4:
                        ln_stats_of(dve, 5 + b, 1 - p, following(b, p))
                    if j == 6:
                        ln_scale(dve, 5 + b, 1 - p, following(b, p))
                    jw = j - LAG
                    if jw >= 0:
                        wd = width(jw)
                        dve.wait_ge(c_mm, FC * b + jw + 1)
                        need(dve, up_ready, FC * b + jw + 1)
                        need(dve, y_part, FC * b + jw - 2)
                        V.tensor_tensor(HID[0:wd, jw % 3], PS[0:wd, 4], UP[0:wd, jw % 6],
                                        ALU.mult).then_inc(hid_ready, 1)
                need(dve, y_part, FC * b + FC)
                for j in range(2):
                    xs = X[:, tiles(b, 2 * j, 2)]
                    V.tensor_tensor(xs, y_bank(j), xs, ALU.add).then_inc(resid_b, 1)

            def rest1(b, k, bank):
                dve.wait_ge(q_part1, 4 * b + k + 1)
                need(dve, q_part3, 4 * b + k - 1)
                V.tensor_tensor(REST[:, k % 2], PS[:, bank], QP[:, QK_ORDER[k], 0],
                                ALU.subtract).then_inc(q_rest, 1)

            def top(b, q, k):
                dve.wait_ge(top_mm, 64 * b + k + 1)
                V.tensor_reduce(MX[:, q, k // TT, k % TT:k % TT + 1], PS[:, k % 2], AX.X, ALU.max
                                ).then_inc(top_ready, 1)

            def negate(b, q, g):
                need(dve, top_ready, 64 * b + 16 * g + 16)
                m = MX[:, q, HG * g:HG * (g + 1)]
                part = [NP[:, g % 2, :, n].rearrange("p t h -> p h t") for n in range(3)]
                k0 = 16 * b + 4 * g
                V.tensor_scalar(part[0], m, -1.0, None, ALU.mult).then_inc(neg_step, 1)
                dve.wait_ge(neg_step, k0 + 1)
                V.scalar_tensor_tensor(NREM[:], m, -1.0, part[0], ALU.mult, ALU.subtract).then_inc(neg_step, 1)
                dve.wait_ge(neg_step, k0 + 2)
                V.tensor_copy(part[1], NREM[:]).then_inc(neg_step, 1)
                dve.wait_ge(neg_step, k0 + 3)
                V.tensor_tensor(part[2], NREM[:], part[1], ALU.subtract).then_inc(neg_step, 1)

            def add_c(b):
                for j in range(2):
                    dve.wait_ge(wo_mm, 2 * b + j + 1)
                    xs = X[:, tiles(b, 2 * j, 2)]
                    V.tensor_tensor(xs, PS[:, 6 + j].rearrange("p (t c) -> p t c", t=2), xs, ALU.add
                                    ).then_inc(resid_c, 1)

            def normalise(b, g):
                dve.wait_ge(ut_mm, 4 * b + g + 1)
                ut = MISC.rearrange("p (t h d) -> p t h d", t=TT, h=HG)
                V.reciprocal(RECIP[:, g % 2], ut[:, :, :, HD]).then_inc(recip_ready, 1)
                dve.wait_ge(recip_ready, 4 * b + g + 1)
                V.tensor_tensor(OTOK[:, :, HG * g:HG * (g + 1)], ut[:, :, :, 0:HD],
                                RECIP[:, g % 2].unsqueeze(3).broadcast_to([P, TT, HG, HD]),
                                ALU.mult).then_inc(otok_ready, 1)

            need(dve, resid_b, 2 * B)
            ln_stats_of(dve, 9, 1, 1)
            for b in range(2):
                for k in range(4):
                    rest1(b, k, 2 + k)
                    if k == 1 and b == 0:
                        ln_scale(dve, 9, 1, 1)
            for g in range(GR):
                for k in range(16):
                    top(0, 0, 16 * g + k)
                negate(0, 0, g)
            for b, p, i, left in attention_batches(dve):
                src = b + 2 if left == 2 else 0
                if left == 1:
                    hold(dve, resid_c, 2)
                for s in range(STEPS):
                    if left:
                        top(b + 1, 1 - p, 4 * s)
                        for k in range(1, 4):
                            top(b + 1, 1 - p, 4 * s + k)
                        if left == 2 and s in QK_STEPS:
                            rest1(b + 2, QK_STEPS.index(s), 7)
                        if s == 0:
                            ln_stats_of(dve, b + 10, p, src)
                        if s == 1:
                            ln_scale(dve, b + 10, p, src)
                        if s % 4 == 3:
                            negate(b + 1, 1 - p, s // 4)
                    if s in OUT_STEPS:
                        normalise(b, OUT_STEPS.index(s))
                normalise(b, GR - 1)
                dve.wait_ge(ob_mm, 2 * b + 2)
                V.tensor_copy(OT[:, 1], PS[:, 3]).then_inc(o_ready, 1)
                add_c(b)

            def x_parts(b, q):
                dve.wait_ge(xnt_ready, 2 * b + 26)
                V.tensor_tensor(XR[:, q], XNT[:, q], XNT[:, q].bitcast(bf16)[:, :, 1:2 * T:2],
                                ALU.subtract).then_inc(x_rem, 1)
                dve.wait_ge(x_rem, b + 1)
                V.tensor_tensor(X3[:, q], XR[:, q], XR[:, q].bitcast(bf16)[:, :, 1:2 * T:2],
                                ALU.subtract).then_inc(x_part3, 1)

            need(dve, resid_c, 2 * B)
            x_parts(0, 0)
            for b, p in batches(dve):
                hold(dve, resid_d, 2 * b)
                for j in range(DC):
                    need(dve, ge_ready, DC * b + j + 1)
                    need(dve, yf_part, DC * b + j - 2)
                    V.tensor_tensor(GREM[:, j % 3], GE[:, j % 3], GE[:, j % 3].bitcast(bf16)[:, 1:2 * T:2],
                                    ALU.subtract).then_inc(g_rem, 1)
                    if j == 0:
                        ln_stats_of(dve, 13 + b, 1 - p, following(b, p))
                    if j == 2:
                        ln_scale(dve, 13 + b, 1 - p, following(b, p))
                x_parts(b + 1, 1 - p)
                need(dve, yf_part, DC * b + DC)
                for j in range(2):
                    xs = X[:, tiles(b, 2 * j, 2)]
                    V.tensor_tensor(xs, y_bank(j), xs, ALU.add).then_inc(resid_d, 1)

        @block.tensor
        def _(pe):
            MM = nc.tensor.matmul
            pe.wait_ge(ident_in, 16)
            for c in range(CT):
                ln_transpose(pe, 0, 0, c)
            pe.wait_ge(w0_in, 32)
            for b, p in batches(pe):
                pe.wait_ge(xnt_ready, 2 * b + 2)
                for k, m in enumerate((0, 2, 1, 3)):
                    need(pe, scan_act, 4 * b + k - 3)
                    for c in range(CT):
                        mm = MM(PS[:, m], W0[:, c, m * P:(m + 1) * P], XNT[:, p, c], start=c == 0, stop=c == CT - 1)
                    mm.then_inc(scan_mm, 1)
                for c in range(CT):
                    ln_transpose(pe, b + 1, 1 - p, c)
                pe.wait_ge(scanned, 2 * b + 2)
                need(pe, resid_a, 2 * b)
                for t in range(TT):
                    for c in range(CT):
                        mm = nc.tensor.transpose(PS[:, 4 + t // 2, (t % 2) * C + c * P:(t % 2) * C + (c + 1) * P],
                                                 HS[:, p, c, t * P:(t + 1) * P], IDENT[:])
                    if t % 2:
                        mm.then_inc(back_mm, 1)
            pe.wait_ge(ones_set, 1)
            pe.wait_ge(xnt_ready, 10)
            pe.wait_ge(wabs, 2)
            MM(MISC[:, 0:2], ONES[:], WSUM[:], start=True, stop=True).then_inc(wtot, 1)
            pe.wait_ge(mix_in, 64)
            pe.wait_ge(const_in, 48)
            pe.wait_ge(wstep, 1)
            for b, p in batches(pe):
                pe.wait_ge(xnt_ready, 2 * b + 10)
                for c in range(CT):
                    mm = MM(MISC[0:NG], GATE[:, c], XNT[:, p, c], start=c == 0, stop=c == CT - 1)
                mm.then_inc(logit_mm, 1)
                for j in range(FC + LAG + 1):
                    if j < FC:
                        wd = width(j)
                        need(pe, silu_ready, FC * b + j - 1)
                        for c in range(CT):
                            mm = MM(PS[0:wd, j % 2], FC1[:, c, j * P:j * P + wd], XNT[:, p, c],
                                    start=c == 0, stop=c == CT - 1)
                        mm.then_inc(h1_mm, 1)
                        need(pe, up_ready, FC * b + j - 1)
                        for c in range(CT):
                            mm = MM(PS[0:wd, 2 + j % 2], FC2[:, c, j * P:j * P + wd], XNT[:, p, c],
                                    start=c == 0, stop=c == CT - 1)
                        mm.then_inc(h2_mm, 1)
                    if j == 0:
                        hold(pe, logit_sb, b + 1)
                        for t in range(TT):
                            mm = nc.tensor.transpose(MISC[:, 16 * t:16 * t + NG], LOGIT[:, t * P:(t + 1) * P],
                                                     IDENT[0:NG, 0:NG])
                        mm.then_inc(logit_t, 1)
                    if j == 2:
                        pe.wait_ge(comb_step, 3 * b + 3)
                        for t in range(TT):
                            mm = nc.tensor.transpose(MISCB[0:3 * NG, t * P:(t + 1) * P],
                                                     CPART[:, t].rearrange("p n e -> p (n e)"), IDENTB[:])
                        mm.then_inc(comb_mm, 1)
                    if j in (8, 9):
                        ln_transpose(pe, 5 + b, 1 - p, j - 8)
                    jc = j - LAG
                    if 0 <= jc < FC:
                        if jc == 0:
                            pe.wait_ge(comb_ready, b + 1)
                            need(pe, resid_a, 2 * B)
                        need(pe, hid_ready, FC * b + jc)
                        MM(PS[0:width(jc), 4], SEL[:, jc * P:jc * P + width(jc)], COMBT[:, p],
                           start=True, stop=True).then_inc(c_mm, 1)
                    jp = jc - 1
                    if jp >= 0:
                        wd = width(jp)
                        if jp == 0:
                            need(pe, resid_b, 2 * b)
                        need(pe, hid_ready, FC * b + jp + 1)
                        for t in range(TT):
                            mm = MM(y_bank(t // 2)[:, t % 2], HID[0:wd, jp % 3, t * P:(t + 1) * P],
                                    PROJ[0:wd, jp], start=jp == 0 and t % 2 == 0, stop=jp == FC - 1,
                                    skip_group_check=True)
                        mm.then_inc(y_part, 1)

            def qk_project(b, q, k, bank):
                w = QK_ORDER[k]
                for c in range(CT):
                    mm = MM(PS[:, bank], (WQ, WK)[w // 2][:, c, (w % 2) * P:(w % 2 + 1) * P], XNT[:, q, c],
                            start=c == 0, stop=c == CT - 1)
                mm.then_inc(q_mm, 1)

            def v_project(b, q, j):
                for t in (2 * j, 2 * j + 1):
                    for c in range(CT):
                        mm = MM(PS[:, j, (t % 2) * C:(t % 2 + 1) * C], XNT[:, q, c, t * P:(t + 1) * P],
                                WV[:, c], start=c == 0, stop=c == CT - 1)
                mm.then_inc(v_mm, 1)

            def top_scores(b, q, k):
                h, t = divmod(k, TT)
                need(pe, top_ready, 64 * b + k - 1)
                MM(PS[:, k % 2], QS[q][0:KROWS, h, t * P:(t + 1) * P], KS[q][0:KROWS, h],
                   start=True, stop=True).then_inc(top_mm, 1)

            def neg_transpose(b, g):
                pe.wait_ge(neg_step, 16 * b + 4 * g + 4)
                for t in range(TT):
                    mm = nc.tensor.transpose(MISCB[0:3 * HG, t * P:(t + 1) * P],
                                             NP[:, g % 2, t].rearrange("p n h -> p (n h)"), IDENTB[:])
                mm.then_inc(neg_t, 1)

            def scores(b, q, s, j):
                g, kt = divmod(s, TT)
                need(pe, exp_done, 32 * b + 2 * s + j - 1)
                for k in range(2):
                    mm = MM(PS[:, 2 + 2 * j + k], KS[q][0:MROWS, HG * g + 2 * j + k, kt * P:(kt + 1) * P],
                            QS[q][0:MROWS, HG * g + 2 * j + k], start=True, stop=True)
                mm.then_inc(s_mm, 1)

            def weigh(b, q, s):
                g, kt = divmod(s, TT)
                need(pe, exp_done, 32 * b + 2 * s + 2)
                if kt == 0:
                    need(pe, u_ready, 4 * b + g)
                for k in range(HG):
                    mm = MM(PS[32 * k:32 * k + 32, 6], VA[:, q, kt, HG * g + k], PR[:, kt % 2, k],
                            start=kt == 0, stop=kt == TT - 1)
                mm.then_inc(pv_done, 1)

            def turn_output(b, g):
                need(pe, u_ready, 4 * b + g + 1)
                for t in range(TT):
                    mm = nc.tensor.transpose(MISC[:, t * P:(t + 1) * P], U[:, g % 2, t * P:(t + 1) * P], IDENT[:])
                mm.then_inc(ut_mm, 1)

            def turn_back(c):
                for t in range(TT):
                    mm = nc.tensor.transpose(PS[:, 2 + c, t * P:(t + 1) * P],
                                             OTOK[:, t, c * H // 2:(c + 1) * H // 2].rearrange("p h d -> p (h d)"),
                                             IDENT[:])
                mm.then_inc(ob_mm, 1)

            def out_project(b, j):
                for t in (2 * j, 2 * j + 1):
                    for c in range(CT):
                        mm = MM(PS[:, 6 + j, (t % 2) * C:(t % 2 + 1) * C], OT[:, c, t * P:(t + 1) * P],
                                WO[:, c], start=c == 0, stop=c == CT - 1)
                mm.then_inc(wo_mm, 1)

            pe.wait_ge(attn_in, 64)
            pe.wait_ge(k_ones, 32)
            need(pe, resid_b, 2 * B)
            for b in range(2):
                pe.wait_ge(xnt_ready, 2 * b + 18)
                for k in range(4):
                    need(pe, q_rest, 4 * b + k - 3)
                    qk_project(b, b, k, 2 + k)
                for j in range(2):
                    need(pe, v_ready, 2 * b + j - 1)
                    v_project(b, b, j)
                if b == 0:
                    for c in range(CT):
                        ln_transpose(pe, 9, 1, c)
            need(pe, v_ready, 4)
            for g in range(GR):
                if g % 2 == 0:
                    pe.wait_ge(stack_in[0][g // 2], 16 * 12)
                for k in range(16):
                    top_scores(0, 0, 16 * g + k)
                if g:
                    if g > 1:
                        pe.wait_ge(nt_ready, g - 1)
                    neg_transpose(0, g - 1)
            pe.wait_ge(nt_ready, GR - 1)
            neg_transpose(0, GR - 1)
            need(pe, q_rest, 8)
            pe.wait_ge(nt_ready, GR)
            for b, p, i, left in attention_batches(pe):
                free = (resid_c, 2 * b)
                need(pe, resid_c, 2 * b)
                if left:
                    need(pe, v_ready, 2 * b + 4)
                for s in range(STEPS):
                    g, kt = divmod(s, TT)
                    if left:
                        if s % 8 == 0:
                            pe.wait_ge(stack_in[1 - p][s // 8], 16 * 12 * (i + p + 1))
                        top_scores(b + 1, 1 - p, 4 * s)
                    if kt == 0:
                        pe.wait_ge(nm_in[g], 16 * b + 16)
                    scores(b, p, s, 0)
                    if left:
                        top_scores(b + 1, 1 - p, 4 * s + 1)
                    if left and s in LN_STEPS:
                        c = LN_STEPS.index(s)
                        need(pe, *free)
                        ln_transpose(pe, b + 10, p, c)
                        free = (xnt_ready, 2 * b + 20 + c + 1)
                    if s in OUT_STEPS:
                        need(pe, *free)
                        turn_output(b, g - 1)
                        free = (otok_ready, 4 * b + g)
                    if left and s in NEG_STEPS:
                        need(pe, *free)
                        neg_transpose(b + 1, g - 1)
                        free = (nt_ready, 4 * b + 4 + g)
                    if left == 2 and s in QK_STEPS:
                        k = QK_STEPS.index(s)
                        need(pe, *free)
                        if k == 0:
                            pe.wait_ge(xnt_ready, 2 * b + 22)
                        qk_project(b + 2, p, k, 7)
                        free = (q_rest, 4 * b + 8 + k + 1)
                    if left:
                        top_scores(b + 1, 1 - p, 4 * s + 2)
                    scores(b, p, s, 1)
                    if s:
                        weigh(b, p, s - 1)
                    if left:
                        top_scores(b + 1, 1 - p, 4 * s + 3)
                weigh(b, p, STEPS - 1)
                if left:
                    need(pe, top_ready, 64 * b + 128)
                if left == 2:
                    v_project(b + 2, p, 0)
                need(pe, *free)
                turn_output(b, GR - 1)
                if left == 2:
                    v_project(b + 2, p, 1)
                pe.wait_ge(otok_ready, 4 * b + GR)
                for c in range(CT):
                    turn_back(c)
                if left:
                    neg_transpose(b + 1, GR - 1)
                pe.wait_ge(o_ready, 2 * b + 2)
                out_project(b, 0)
                if left:
                    pe.wait_ge(nt_ready, 4 * b + 4 + GR)
                out_project(b, 1)

            need(pe, resid_c, 2 * B)
            pe.wait_ge(tern_ready, 2)
            for b, p in batches(pe):
                pe.wait_ge(x_part3, b + 1)
                moving = [XNT[:, p].bitcast(bf16)[:, :, 1:2 * T:2], XR[:, p].bitcast(bf16)[:, :, 1:2 * T:2],
                          X3[:, p]]
                for j in range(DC + 2):
                    if j < DC:
                        need(pe, ge_ready, DC * b + j - 1)
                        for c in range(CT):
                            for n in range(3):
                                mm = MM(PS[:, j % 2], W1Q[:, c, j * P:(j + 1) * P], moving[n][:, c],
                                        start=c + n == 0, stop=c == CT - 1 and n == 2)
                        mm.then_inc(ff_mm, 1)
                    if j in (5, 6):
                        ln_transpose(pe, 13 + b, 1 - p, j - 5)
                    jp = j - 2
                    if jp >= 0:
                        if jp == 0:
                            need(pe, resid_d, 2 * b)
                            for t in range(TT):
                                MM(y_bank(t // 2)[:, t % 2], ONES[0:1], B2[:], start=t % 2 == 0, stop=False,
                                   skip_group_check=True)
                        pe.wait_ge(g_part3, DC * b + jp + 1)
                        left = [GE[:, jp % 3].bitcast(bf16)[:, 1:2 * T:2], GREM[:, jp % 3].bitcast(bf16)[:, 1:2 * T:2],
                                G3[:, jp % 3]]
                        for t in range(TT):
                            for n in range(3):
                                mm = MM(y_bank(t // 2)[:, t % 2], left[n][:, t * P:(t + 1) * P], W2Q[:, jp],
                                        start=False, stop=jp == DC - 1 and n == 2,
                                        skip_group_check=True)
                        mm.then_inc(yf_part, 1)


_OUT = (B, T, C)


def kernel(L0_attn_x, L0_attn_W, L0_attn_b, L0_ffn_gate_w, L0_ffn_expert_fc1, L0_ffn_expert_fc2,
           L0_ffn_expert_proj, L0_ffn_shared_fc1, L0_ffn_shared_fc2, L0_ffn_shared_proj,
           L0_ffn_shared_gate_w, L1_attn_Wq, L1_attn_Wk, L1_attn_Wv, L1_attn_Wo, L1_ffn_w1, L1_ffn_b1,
           L1_ffn_w2, L1_ffn_b2):
    import ml_dtypes
    import numpy as np
    import concourse.bacc as bacc
    from concourse.bass_utils import run_bass_kernel_spmd

    def a(v):
        return np.asarray(v)

    def rows(w):
        wt = a(w).T
        return np.ascontiguousarray(wt.reshape(-1, P, wt.shape[1]).transpose(1, 0, 2))

    fc1 = np.concatenate([a(L0_ffn_expert_fc1).reshape(NE * FE, C), a(L0_ffn_shared_fc1)])
    fc2 = np.concatenate([a(L0_ffn_expert_fc2).reshape(NE * FE, C), a(L0_ffn_shared_fc2)])
    pj = np.concatenate([a(L0_ffn_expert_proj).transpose(0, 2, 1).reshape(NE * FE, C),
                         a(L0_ffn_shared_proj).T])
    pj = np.concatenate([pj, np.zeros((FC * P - F, C), pj.dtype)])
    expert_of = np.minimum(np.arange(F) // FE, NE)
    low = np.arange(NE)[None, :] < np.arange(NE)[:, None]
    data = {
        "x": a(L0_attn_x),
        "w0": rows(L0_attn_W),
        "b0": np.ascontiguousarray(a(L0_attn_b).reshape(4, P).T),
        "fc1": rows(fc1), "fc2": rows(fc2),
        "proj": np.ascontiguousarray(pj.reshape(FC, P, C).transpose(1, 0, 2)),
        "gate": rows(np.concatenate([a(L0_ffn_gate_w), a(L0_ffn_shared_gate_w)])),
        "sel": np.tile(np.arange(NG)[:, None] == expert_of[None, :], (3, 1)).astype(ml_dtypes.bfloat16),
        "wq": rows(L1_attn_Wq), "wk": rows(L1_attn_Wk), "wv": rows(L1_attn_Wv),
        "wo": rows(L1_attn_Wo),
        "w1": rows(L1_ffn_w1),
        "b1": np.ascontiguousarray(a(L1_ffn_b1).reshape(DC, P).T),
        "w2": rows(L1_ffn_w2),
        "b2": a(L1_ffn_b2)[None],
        "ident": np.eye(P, dtype=np.float32),
        "identb": np.eye(P, dtype=np.float32).astype(ml_dtypes.bfloat16),
        "kones": np.ones((MROWS - KROWS, H, T), ml_dtypes.bfloat16),
        "lower": np.ascontiguousarray(np.broadcast_to(low, (P, NE, NE))).astype(np.float32),
    }
    nc = bacc.Bacc("TRN2", target_bir_lowering=False, num_devices=1)
    arrays, args = {}, {}
    for name, v in data.items():
        arrays[f"in_{name}"] = v
        args[name] = nc.dram_tensor(f"in_{name}", v.shape, mybir.dt.from_np(v.dtype), kind="ExternalInput").ap()
    args["out"] = nc.dram_tensor("out_0", _OUT, mybir.dt.float32, kind="ExternalOutput").ap()
    build(nc, **args)
    r = run_bass_kernel_spmd(nc, [arrays], core_ids=[0])
    return r.results[0]["out_0"]
```

```python
import concourse.bass as bass
from concourse import mybir
from contextlib import ExitStack

B, T, C = 4, 512, 256
P = 128
CT = C // P
TT = T // P
NE, TOPK = 8, 2
FE, FS = 176, 704
F = NE * FE + FS
FC = -(-F // P)
NG = NE + 1
H, HD = 16, 16
HG = 4
GR = H // HG
DFF = 1024
DC = DFF // P
EPS = 1e-5
PAIRS = B // 2
FCW = 2 * CT * P
GROUPS = (0, 2, 7, 12, FC)
DLAG = 4
XNORM2 = C
GEXP = 14
TOPEXP = 13
LAG = 5
QPART, KPART = (0, 0, 1, 1, 0, 2), (0, 1, 0, 1, 2, 0)
KROWS = HD * len(QPART)
MROWS = KROWS + 3
QK_ORDER = (0, 2, 1, 3)
STEPS = GR * TT
LN_STEPS, OUT_STEPS, NEG_STEPS, QK_STEPS = (3, 4), (5, 9, 13), (6, 10, 14), (7, 8, 11, 12)
ABS_AT = (1, 2, 3, 4)
LN8_AT = (11, 12)
QK0_AT = (14, 15, 16, 17)
NEG0_AT = (10, 13, 17, 20)
QK1_AT = (18, 19, 20, 21)
TOP_FROM = LAG
TOP_PER, TOP_PER_SIDE = 5, 4


def ln_at(left):
    return (11, 14) if left == 0 else (8, 9)


def tops_at(j):
    def until(j):
        return min(H * TT, sum(TOP_PER_SIDE if m in NEG0_AT + ln_at(0) else TOP_PER for m in range(TOP_FROM, j)))
    banks = (4, 7, 7, 7) if j in NEG0_AT + ln_at(0) else (7, 4, 7, 7, 7)
    return list(zip(range(until(j), until(j + 1)), banks))


def width(j):
    return min(P, F - j * P)


def build(nc, x, w0, b0, fc, proj, gate, sel, wq, wk, wv, wo, w1, b1, w2, b2,
          ident, identb, kones, lower, out):
    f32, bf16, f16, i32 = mybir.dt.float32, mybir.dt.bfloat16, mybir.dt.float16, mybir.dt.int32
    ALU, ACT, AX = mybir.AluOpType, mybir.ActivationFunctionType, mybir.AxisListType

    ctx = ExitStack()
    with ctx:
        def sb(name, shape, dt):
            return ctx.enter_context(nc.sbuf_tensor(name, shape, dt))

        def sem(name):
            return ctx.enter_context(nc.semaphore(name))

        X = sb("X", [P, B * TT, C], f32)
        XN = sb("XN", [P, 2, TT, C], f32)
        XNT = sb("XNT", [P, 2, CT, T], f32)
        STATS = sb("STATS", [P, 2, TT, 6], f32)
        MV = sb("MV", [P, 2, TT, 2], f32)
        VE = sb("VE", [P, 2, TT], f32)
        RSTD = sb("RSTD", [P, 2, TT], f32)
        MHALF = sb("MHALF", [P, TT], f32)
        IDENT = sb("IDENT", [P, P], f32)
        IDENTB = sb("IDENTB", [P, P], bf16)
        LOWER = sb("LOWER", [P, NE, NE], f32)
        ONES = sb("ONES", [P, P], f32)
        SEL = sb("SEL", [3 * NG, F], bf16)
        B0 = sb("B0", [P, 4], f32)
        GATE = sb("GATE", [P, CT, NG], f32)
        WQ = sb("WQ", [P, CT, C], f32)
        WK = sb("WK", [P, CT, C], f32)
        WV = sb("WV", [P, CT, C], f32)
        WO = sb("WO", [P, CT, C], f32)
        B1 = sb("B1", [P, DC], f32)
        B2 = sb("B2", [P, C], f32)
        BMAX = sb("BMAX", [P, 1], f32)
        GMAX = sb("GMAX", [P, 2], f32)
        GSC = sb("GSC", [P, 2], f32)
        W1Q = sb("W1Q", [P, CT, DFF], f16)
        W2Q = sb("W2Q", [P, DC, C], f16)

        HT2 = H * T // 2
        BIG = sb("BIG", [P, FC * (FCW + C) + HT2], f32)
        FCRAW = BIG[:, 0:FC * FCW]
        FCL = BIG[:].bitcast(f16)[:, 0:FC * FCW]
        PROJ = BIG[:, FC * FCW:FC * (FCW + C)].rearrange("p (j c) -> p j c", j=FC)
        QS = [BIG[:, c:c + HT2].bitcast(bf16).rearrange("p (h t) -> p h t", h=H) for c in (FC * (FCW + C), 0)]
        KS = [BIG[:, c:c + HT2].bitcast(bf16).rearrange("p (h t) -> p h t", h=H) for c in (FC * FCW // 2, FC * FCW)]

        WORKA = sb("WORKA", [P, 12 * T], f32)
        GV = WORKA[:, 0:8 * T].rearrange("p (b m t) -> p b m t", b=2, m=4)
        HS = WORKA[:, 8 * T:12 * T].rearrange("p (b m t) -> p b m t", b=2, m=CT)
        SILU = WORKA[:, 0:2 * T].rearrange("p (r t) -> p r t", r=2)
        UP = WORKA[:, 2 * T:9 * T].rearrange("p (r t) -> p r t", r=LAG + 2)
        HID = WORKA[:, 9 * T:12 * T].rearrange("p (r t) -> p r t", r=3)
        PR = WORKA[:, 0:8 * T].rearrange("p (r h t) -> p r h t", r=2, h=HG)
        WORKB = sb("WORKB", [P, 8 * T], f32)
        RAW1 = WORKB[:, 0:4 * T].rearrange("p (k f) -> p k f", k=CT)
        RAW2 = WORKB[:, 4 * T:8 * T].rearrange("p (k f) -> p k f", k=DC)
        VA = WORKB[:, :].rearrange("p (b t h d) -> p b t h d", b=2, t=TT, h=H)
        WORKC = sb("WORKC", [P, 16 * T], f32)
        W0 = WORKC[:, 14 * T:16 * T].rearrange("p (k f) -> p k f", k=CT)
        QP = WORKC[:, 0:6 * T].bitcast(bf16).rearrange("p (w n t) -> p w n t", w=4, n=3)
        REST = WORKC[:, 6 * T:8 * T].rearrange("p (r t) -> p r t", r=2)
        QP0 = WORKB[:, 0:6 * T].bitcast(bf16).rearrange("p (w n t) -> p w n t", w=4, n=3)
        REST0 = WORKB[:, 6 * T:8 * T].rearrange("p (r t) -> p r t", r=2)
        U = WORKC[:, 8 * T:10 * T].rearrange("p (r t) -> p r t", r=2)
        OTOK = WORKC[:, 10 * T:12 * T].rearrange("p (t h d) -> p t h d", t=TT, h=H)
        OT = WORKA[:, 8 * T:10 * T].rearrange("p (c t) -> p c t", c=CT)
        NT = WORKC[:, 14 * T:15 * T].bitcast(bf16).rearrange("p (r t) -> p r t", r=2)
        FCH = WORKC[:, 0:FC * FCW // 2].bitcast(f16)
        XH = WORKC[:, 12 * T:14 * T].bitcast(f16).rearrange("p (b k t) -> p b k t", b=2, k=CT)
        XL = WORKC[:, 14 * T:16 * T].bitcast(f16).rearrange("p (b k t) -> p b k t", b=2, k=CT)
        TERN = WORKC[:, 9 * T:11 * T]
        GE = WORKC[:, 0:5 * T].rearrange("p (r t) -> p r t", r=DLAG + 1)
        GH = WORKC[:, 5 * T:15 * T // 2].bitcast(f16).rearrange("p (r t) -> p r t", r=DLAG + 1)
        GL = WORKC[:, 15 * T // 2:10 * T].bitcast(f16).rearrange("p (r t) -> p r t", r=DLAG + 1)

        LOGIT = sb("LOGIT", [NG, T], f32)
        ROWMAX = sb("ROWMAX", [P, TT], f32)
        ZE = sb("ZE", [P, TT, NE], f32)
        ZS = sb("ZS", [P, TT], f32)
        EE = sb("EE", [P, TT, NE], f32)
        ES = sb("ES", [P, TT], f32)
        ESUM = sb("ESUM", [P, TT], f32)
        ERCP = sb("ERCP", [P, TT], f32)
        GT = sb("GT", [P, TT, NE, NE], f32)
        EQ = sb("EQ", [P, TT, NE, NE], f32)
        RANK = sb("RANK", [P, TT, NE], f32)
        SELE = sb("SELE", [P, TT, NE], f32)
        COMB = sb("COMB", [P, TT, NG], f32)
        CREM = sb("CREM", [P, TT, NG], f32)
        CPART = sb("CPART", [P, TT, 3, NG], bf16)
        COMBT = sb("COMBT", [3 * NG, 2, T], bf16)
        MX = sb("MX", [P, 2, H, TT], f32)
        RECIP = sb("RECIP", [P, 2, TT, HG], f32)
        NREM = sb("NREM", [P, HG, TT], f32)
        NP = sb("NP", [P, 2, TT, 3, HG], bf16)
        FMAX = sb("FMAX", [P, B + 1], f32)
        FMAXT = sb("FMAXT", [1, 1], f32)
        FSC = sb("FSC", [1, 2], f32)
        SCALE = sb("SCALE", [P, 2], f32)
        WSUM = sb("WSUM", [P, 4], f32)
        WALL = sb("WALL", [P, 4], f32)
        WTOT = sb("WTOT", [P, 2], f32)
        WMEAN = sb("WMEAN", [P, 2], f32)
        THR = sb("THR", [P, 2], f32)
        NTHR = sb("NTHR", [P, 2], f32)

        PS = ctx.enter_context(nc.psum_tensor("PS", [P, 8, 512], f32))
        MISC = PS[:, 7]
        MISCB = MISC.bitcast(bf16)

        qk_dram = nc.dram_tensor("qk_parts", [B, 4, 3, P, T], bf16, kind="Internal").ap()
        nm_dram = nc.dram_tensor("neg_max_parts", [B, GR, 3 * HG, T], bf16, kind="Internal").ap()

        held = sem("held")
        x_first, x_rest = sem("x_first"), sem("x_rest")
        w0_in, ident_in, const_in, mix_in, attn_in, ffn_in = (sem(n) for n in (
            "w0_in", "ident_in", "const_in", "mix_in", "attn_in", "ffn_in"))
        ones_set, half_set = sem("ones_set"), sem("half_set")
        ln_stats, ln_mv, ln_var, ln_rstd, xn_ready, xnt_psum, xnt_ready = (sem(n) for n in (
            "ln_stats", "ln_mv", "ln_var", "ln_rstd", "xn_ready", "xnt_psum", "xnt_ready"))
        scan_mm, scan_act, scanned, back_mm, resid_a = (sem(n) for n in (
            "scan_mm", "scan_act", "scanned", "back_mm", "resid_a"))
        (logit_mm, logit_sb, logit_t, router_step, comb_step, router_z, router_e, comb_mm, comb_ready,
         h1_mm, h2_mm, silu_ready, up_ready, c_mm, hid_ready, y_part, resid_b) = (sem(n) for n in (
            "logit_mm", "logit_sb", "logit_t", "router_step", "comb_step", "router_z", "router_e", "comb_mm",
            "comb_ready", "h1_mm", "h2_mm", "silu_ready", "up_ready", "c_mm", "hid_ready",
            "y_part", "resid_b"))
        wabs, wstep, above, tern_ready = (sem(n) for n in ("wabs", "wstep", "above", "tern_ready"))
        fc_in, fmax, fmax_t, fscale, fsc_mm, scale_ready, fch_ready, fcl_ready, xh_ready, xl_ready = (
            sem(n) for n in ("fc_in", "fmax", "fmax_t", "fscale", "fsc_mm", "scale_ready",
                             "fch_ready", "fcl_ready", "xh_ready", "xl_ready"))
        (q_mm, q_part1, q_rest, q_part2, q_part3, v_mm, v_ready, k_ones, v_ones, top_mm, top_ready,
         neg_step, neg_t, nt_ready, s_mm, exp_done, pv_done, u_ready, ut_mm, recip_ready, otok_ready,
         ob_mm, o_ready, wo_mm, resid_c) = (sem(n) for n in (
            "q_mm", "q_part1", "q_rest", "q_part2", "q_part3", "v_mm", "v_ready", "k_ones", "v_ones",
            "top_mm", "top_ready", "neg_step", "neg_t", "nt_ready", "s_mm", "exp_done", "pv_done",
            "u_ready", "ut_mm", "recip_ready", "otok_ready", "ob_mm", "o_ready", "wo_mm", "resid_c"))
        parts_out = [sem(f"parts_out{w}") for w in range(4)]
        stack_in = [[sem(f"stack_in{p}{half}") for half in range(2)] for p in range(2)]
        nm_out = [sem(f"nm_out{g}") for g in range(GR)]
        nm_in = [sem(f"nm_in{g}") for g in range(GR)]
        (ff_mm, ge_ready, gh_ready, gl_ready, yf_part, resid_d, stored, gbound, gmax, gscale) = (
            sem(n) for n in ("ff_mm", "ge_ready", "gh_ready", "gl_ready", "yf_part",
                             "resid_d", "stored", "gbound", "gmax", "gscale"))
        b2_added = sem("b2_added")

        CREDIT = {wabs: 1, scan_act: 4, resid_a: 2, silu_ready: 2, up_ready: 2, hid_ready: 1, y_part: 3,
                  resid_b: 2, q_rest: 4, q_part3: 2, top_ready: 2, exp_done: 2, pv_done: 2, v_ready: 2,
                  u_ready: 1, resid_c: 2, ge_ready: 4, yf_part: DLAG + 1, resid_d: 2}
        for w in range(4):
            CREDIT[parts_out[w]] = 16
            CREDIT[nm_out[w]] = 16

        def need(eng, s, n):
            eng.wait_ge(s, n + CREDIT.get(s, 0))

        def hold(eng, s, n):
            need(eng, s, n)
            eng.sem_inc(held, 1)

        def batches(eng):
            with eng.Fori(0, PAIRS) as i:
                for p in range(2):
                    yield 2 * i + p, p

        def following(b, p):
            return b + 1 if p == 0 else B - 1 - b

        def peeled_batches(eng):
            with eng.Fori(0, PAIRS - 1) as i:
                for p in range(2):
                    yield 2 * i + p, p, i, 2
            for p in range(2):
                yield B - 2 + p, p, PAIRS - 1, 1 - p

        def tiles(b, j=0, n=TT):
            return bass.ds(TT * b + j, n)

        def parts_of(b, w):
            return QP0[:, w] if isinstance(b, int) and b == 0 else QP[:, w]

        def rest_of(b, k):
            return REST0[:, k % 2] if isinstance(b, int) and b == 0 else REST[:, k % 2]

        def y_bank(j):
            return PS[:, 5 + j].rearrange("p (t c) -> p t c", t=2)

        def ln_stats_tile(q, src, t):
            nc.vector.bn_stats(STATS[:, q, t], X[:, bass.ds(src * TT + t, 1)]).then_inc(ln_stats, 1)

        def ln_aggregate(dve, n, q):
            hold(dve, ln_stats, 4 * n + 4)
            for t in range(TT):
                nc.vector.bn_aggr(MV[:, q, t], STATS[:, q, t]).then_inc(ln_mv, 1)

        def ln_stats_of(dve, n, q, src):
            for t in range(TT):
                ln_stats_tile(q, src, t)
            ln_aggregate(dve, n, q)

        def ln_rstd_of(pool, n, q):
            hold(pool, ln_mv, 4 * n + 4)
            nc.gpsimd.tensor_scalar(VE[:, q], MV[:, q, :, 1], EPS, None, ALU.add).then_inc(ln_var, 1)
            pool.wait_ge(ln_var, n + 1)
            nc.gpsimd.tensor_tensor(RSTD[:, q], VE[:, q], MHALF[:], ALU.pow).then_inc(ln_rstd, 1)

        def ln_scale_tile(q, src, t):
            nc.vector.tensor_scalar(XN[:, q, t], X[:, bass.ds(src * TT + t, 1)].rearrange("p a c -> p (a c)"),
                                    MV[:, q, t, 0:1], RSTD[:, q, t:t + 1],
                                    ALU.subtract, ALU.mult).then_inc(xn_ready, 1)

        def ln_scale(dve, n, q, src):
            hold(dve, ln_rstd, n + 1)
            for t in range(TT):
                ln_scale_tile(q, src, t)

        def ln_transpose(pe, n, q, c, bank=7):
            pe.wait_ge(xn_ready, TT * n + TT)
            if c == 1 and bank == 7:
                pe.wait_ge(xnt_ready, 2 * n + 1)
            for t in range(TT):
                mm = nc.tensor.transpose(PS[:, bank, t * P:(t + 1) * P], XN[:, q, t, c * P:(c + 1) * P], IDENT[:])
            mm.then_inc(xnt_psum, 1)

        def high_part(act, m, n, q):
            act.wait_ge(xnt_ready, 2 * n + 2)
            nc.scalar.activation(XH[:, q], XNT[:, q], ACT.Copy).then_inc(xh_ready, 1)

        def low_part(dve, m, q):
            dve.wait_ge(xh_ready, m + 1)
            nc.vector.tensor_tensor(XL[:, q], XNT[:, q], XH[:, q], ALU.subtract).then_inc(xl_ready, 1)

        def ln_copy(act, n, q, c, bank=7):
            act.wait_ge(xnt_psum, 2 * n + c + 1)
            nc.scalar.activation(XNT[:, q, c], PS[:, bank], ACT.Copy).then_inc(xnt_ready, 1)

        block = ctx.enter_context(nc.Block())

        @block.sync
        def _(sp):
            for s, n in CREDIT.items():
                sp.sem_inc(s, n)
            xt = x.rearrange("b (t p) c -> b p t c", p=P)
            sp.dma_start(X[:, 0:TT], xt[0]).then_inc(x_first, 16)
            sp.dma_start(IDENT[:], ident).then_inc(ident_in, 16)
            sp.dma_start(W0, w0).then_inc(w0_in, 16)
            sp.dma_start(B0[:], b0).then_inc(w0_in, 16)
            for b in range(1, B):
                sp.dma_start(X[:, b * TT:(b + 1) * TT], xt[b]).then_inc(x_rest, 16)
            sp.dma_start(FCRAW, fc).then_inc(fc_in, 16)
            for dst, src in ((RAW1, w1), (RAW2, w2), (B1[:], b1), (B2[:], b2)):
                sp.dma_start(dst, src).then_inc(ffn_in, 16)
            for dst, src in ((IDENTB, identb), (LOWER, lower), (SEL, sel)):
                sp.dma_start(dst[:], src).then_inc(const_in, 16)
            for dst, src in ((GATE[:], gate), (PROJ, proj)):
                sp.dma_start(dst, src).then_inc(mix_in, 16)
            for dst, src in ((WQ, wq), (WK, wk), (WV, wv), (WO, wo)):
                sp.dma_start(dst[:], src).then_inc(attn_in, 16)

            def parts(b, k):
                w = QK_ORDER[k]
                need(sp, q_part3, 4 * b + k + 1)
                sp.dma_start(qk_dram[bass.ds(b, 1), w].rearrange("a n p t -> p (a n) t"),
                             parts_of(b, w)).then_inc(parts_out[w], 16)

            def stack(b, q, half):
                for w, part, dst in ((half, QPART, QS[q]), (2 + half, KPART, KS[q])):
                    need(sp, parts_out[w], 16 * b + 16)
                    h0 = half * (H // 2)
                    for g, n in enumerate(part):
                        sp.dma_start(dst[HD * g:HD * (g + 1), h0:h0 + H // 2],
                                     qk_dram[bass.ds(b, 1), w, n].rearrange("a (h d) t -> d (a h) t", d=HD)
                                     ).then_inc(stack_in[q][half], 16)

            def neg_rows(b, g, q):
                sp.wait_ge(nt_ready, 4 * b + g + 1)
                sp.dma_start(nm_dram[bass.ds(b, 1), g].rearrange("a r t -> (a r) t"),
                             NT[0:3 * HG, g % 2]).then_inc(nm_out[g], 16)
                need(sp, nm_out[g], 16 * b + 16)
                sp.dma_start(QS[q][KROWS:MROWS, HG * g:HG * (g + 1)],
                             nm_dram[bass.ds(b, 1), g].rearrange("a (n h) t -> (a n) h t", n=3)
                             ).then_inc(nm_in[g], 16)

            for k in range(4):
                parts(0, k)
                if k == 0:
                    sp.dma_start(KS[0][KROWS:MROWS], kones).then_inc(k_ones, 16)
                if k % 2:
                    stack(0, 0, k // 2)
            for g in range(GR):
                neg_rows(0, g, 0)
            for k in range(2):
                parts(1, k)
            need(sp, resid_b, 2 * B)
            stack(1, 1, 0)
            sp.dma_start(KS[1][KROWS:MROWS], kones).then_inc(k_ones, 16)
            for k in range(2, 4):
                parts(1, k)
            stack(1, 1, 1)
            for b, p, i, left in peeled_batches(sp):
                for g in range(GR):
                    if left == 2 and g == GR - 1:
                        need(sp, s_mm, 32 * b + 32)
                        stack(b + 2, p, 1)
                    if left:
                        neg_rows(b + 1, g, 1 - p)
                    if left == 2 and g < 2:
                        parts(b + 2, 2 * g)
                        parts(b + 2, 2 * g + 1)
                        if g == 0:
                            need(sp, s_mm, 32 * b + 16)
                            stack(b + 2, p, 0)
            ot = out.rearrange("b (h t p) c -> (b h) p t c", h=2, p=P)
            with sp.Fori(0, 2 * B) as h:
                need(sp, resid_d, h + 1)
                sp.dma_start(ot[bass.ds(h, 1)].rearrange("a p t c -> p (a t) c"),
                             X[:, bass.ds(2 * h, 2)]).then_inc(stored, 16)
            sp.wait_ge(stored, 16 * 2 * B)

        @block.gpsimd
        def _(pool):
            nc.gpsimd.memset(MHALF[:], -0.5).then_inc(half_set, 1)
            nc.gpsimd.memset(ONES[:], 1.0).then_inc(ones_set, 1)
            pool.wait_ge(half_set, 1)
            ln_rstd_of(pool, 0, 0)
            for b, p in batches(pool):
                ln_rstd_of(pool, b + 1, 1 - p)
            def part3(b, k):
                qp = parts_of(b, QK_ORDER[k])
                pool.wait_ge(q_part2, 4 * b + k + 1)
                nc.gpsimd.tensor_tensor(qp[:, 2], rest_of(b, k), qp[:, 1], ALU.subtract).then_inc(q_part3, 1)

            def thresholds():
                need(pool, wabs, len(ABS_AT))
                nc.gpsimd.partition_all_reduce(WALL[:], WSUM[:], P, bass.bass_isa.ReduceOp.add).then_inc(wstep, 1)
                pool.wait_ge(wstep, 1)
                nc.gpsimd.tensor_tensor(WTOT[:], WALL[:, 0:4:2], WALL[:, 1:4:2], ALU.add).then_inc(wstep, 1)
                for k, (dst, src, factor) in enumerate(((WMEAN, WTOT, 1.0 / (C * DFF)), (THR, WMEAN, 0.7),
                                                        (NTHR, THR, -1.0)), 2):
                    pool.wait_ge(wstep, k)
                    nc.gpsimd.tensor_scalar(dst[:], src[:], factor, None, ALU.mult).then_inc(wstep, 1)
                hold(pool, wstep, 5)

            def ternary(k):
                raw, tern = ((RAW1, W1Q), (RAW2, W2Q))[k]
                raw, tern = raw.rearrange("p k f -> p (k f)"), tern[:].rearrange("p k f -> p (k f)")
                for half in range(2):
                    part, m = slice(2 * T * half, 2 * T * (half + 1)), 2 * k + half
                    if m:
                        hold(pool, tern_ready, m)
                    nc.gpsimd.tensor_scalar(TERN, raw[:, part], THR[:, k:k + 1], None, ALU.is_ge
                                            ).then_inc(above, 1)
                    nc.gpsimd.tensor_scalar(raw[:, part], raw[:, part], NTHR[:, k:k + 1], None, ALU.is_le
                                            ).then_inc(above, 1)
                    pool.wait_ge(above, 2 * m + 2)
                    nc.gpsimd.tensor_tensor(tern[:, part], TERN, raw[:, part], ALU.subtract
                                            ).then_inc(tern_ready, 1)

            for b, p, i, left in peeled_batches(pool):
                if left:
                    ln_rstd_of(pool, b + 5, 1 - p)
                if left == 1:
                    ln_rstd_of(pool, 8, 0)
                    thresholds()
                    for k in range(2):
                        ternary(k)
                    for k in range(4):
                        part3(0, k)
                if left == 0:
                    ln_rstd_of(pool, 9, 1)
            for w in range(4):
                need(pool, parts_out[w], 16)
            for p in range(2):
                nc.gpsimd.memset(VA[:, p, :, :, HD:2 * HD], 1.0).then_inc(v_ones, 1)
            for k in range(4):
                part3(1, k)
            pool.wait_ge(gbound, 1)
            nc.gpsimd.partition_all_reduce(GMAX[:, 0:1], BMAX[:], P, bass.bass_isa.ReduceOp.max).then_inc(gmax, 1)
            for b, p, i, left in peeled_batches(pool):
                if left:
                    ln_rstd_of(pool, b + 10, p)
                if left == 2:
                    for k in range(4):
                        part3(b + 2, k)
            for b, p in batches(pool):
                ln_rstd_of(pool, 13 + b, 1 - p)

        @block.scalar
        def _(act):
            for c in range(CT):
                ln_copy(act, 0, 0, c, 7 - c)
            act.wait_ge(w0_in, 32)
            for b, p in batches(act):
                for k, m in enumerate((0, 2, 1, 3)):
                    act.wait_ge(scan_mm, 4 * b + k + 1)
                    nc.scalar.activation(GV[:, p, m], PS[:, m], ACT.Sigmoid if m < 2 else ACT.Tanh,
                                         bias=B0[:, m:m + 1]).then_inc(scan_act, 1)
                for c in range(CT):
                    ln_copy(act, b + 1, 1 - p, c, 7 - c)
            def part1(b, k, bank):
                w = QK_ORDER[k]
                act.wait_ge(q_mm, 4 * b + k + 1)
                need(act, parts_out[w], 16 * b)
                nc.scalar.activation(parts_of(b, w)[:, 0], PS[:, bank], ACT.Copy).then_inc(q_part1, 1)

            def part2(b, k):
                need(act, q_rest, 4 * b + k + 1)
                nc.scalar.activation(parts_of(b, QK_ORDER[k])[:, 1], rest_of(b, k), ACT.Copy).then_inc(q_part2, 1)

            def v_copy(b, q, j):
                act.wait_ge(v_mm, 2 * b + j + 1)
                nc.scalar.activation(VA[:, q, 2 * j:2 * j + 2, :, 0:HD],
                                     PS[:, j].rearrange("p (t h d) -> p t h d", t=2, h=H),
                                     ACT.Copy).then_inc(v_ready, 1)

            def nt_copy(b, g):
                act.wait_ge(neg_t, 4 * b + g + 1)
                need(act, nm_out[(g + 2) % GR], 16 * b + 16 * (g // 2))
                nc.scalar.activation(NT[0:3 * HG, g % 2], MISCB[0:3 * HG, 0:T], ACT.Copy).then_inc(nt_ready, 1)

            def exps(b, s, j):
                act.wait_ge(s_mm, 32 * b + 2 * s + j + 1)
                if j == 0:
                    need(act, pv_done, 16 * b + s - 1)
                nc.scalar.activation(PR[:, s % 2, 2 * j:2 * j + 2],
                                     PS[:, 2 + 2 * j:4 + 2 * j], ACT.Exp, scale=0.25).then_inc(exp_done, 1)

            def u_copy(b, g):
                need(act, pv_done, 16 * b + 4 * g + 4)
                nc.scalar.activation(U[:, g % 2], PS[:, 6], ACT.Copy).then_inc(u_ready, 1)

            high_part(act, 0, 4, 0)
            act.wait_ge(scale_ready, 1)
            for j0, j1 in zip(GROUPS, GROUPS[1:]):
                part = slice(FCW * j0, FCW * j1)
                nc.scalar.activation(FCH[:, part], FCRAW[:, part], ACT.Copy, scale=SCALE[:, 0:1]
                                     ).then_inc(fch_ready, 1)
            for b, p, i, left in peeled_batches(act):
                act.wait_ge(logit_mm, b + 1)
                nc.scalar.activation(LOGIT[:], MISC[0:NG], ACT.Copy).then_inc(logit_sb, 1)
                for j in range(FC + LAG + 1):
                    if j == LAG:
                        act.wait_ge(comb_mm, b + 1)
                        nc.scalar.activation(COMBT[:, p], MISCB[0:3 * NG, 0:T], ACT.Copy).then_inc(comb_ready, 1)
                    if left and j in ln_at(left):
                        ln_copy(act, 5 + b, 1 - p, ln_at(left).index(j))
                    if left and j == 10:
                        high_part(act, b + 1, 5 + b, 1 - p)
                    if left == 1 and j in LN8_AT:
                        ln_copy(act, 8, 0, LN8_AT.index(j))
                    if left == 1 and j in QK0_AT:
                        act.wait_ge(tern_ready, 4)
                        part1(0, QK0_AT.index(j), 7)
                    if left == 1 and j - 1 in QK0_AT:
                        part2(0, QK0_AT.index(j - 1))
                    if j >= FC:
                        if left == 0 and j in NEG0_AT:
                            nt_copy(0, NEG0_AT.index(j))
                        if left == 0 and j in QK1_AT:
                            k = QK1_AT.index(j)
                            part1(1, k, k)
                            if k:
                                part2(1, k - 1)
                        continue
                    act.wait_ge(h1_mm, FC * b + j + 1)
                    need(act, up_ready, FC * b + j - 1)
                    nc.scalar.activation(SILU[0:width(j), j % 2], PS[0:width(j), j % 2], ACT.Silu,
                                         scale=SCALE[0:width(j), 1:2]).then_inc(silu_ready, 1)
                    if left == 0 and j in ln_at(0):
                        ln_copy(act, 9, 1, ln_at(0).index(j))
                    if left == 0 and j in NEG0_AT:
                        nt_copy(0, NEG0_AT.index(j))
                    if j == 0:
                        act.wait_ge(router_z, 2 * b + 2)
                        nc.scalar.activation(EE[:], ZE[:], ACT.Exp).then_inc(router_e, 1)
                        nc.scalar.activation(ES[:], ZS[:], ACT.Exp, scale=-1.0).then_inc(router_e, 1)
                    if left == 1 and j in ABS_AT:
                        m = ABS_AT.index(j)
                        act.wait_ge(ffn_in, 64)
                        need(act, wabs, m)
                        nc.scalar.activation(TERN.bitcast(bf16)[:, 0:2 * T], WORKB[:, 2 * T * m:2 * T * (m + 1)],
                                             ACT.Abs, accum_out=WSUM[:, m:m + 1]).then_inc(wabs, 1)

            part2(1, 3)
            act.wait_ge(v_ones, 2)
            for b in range(2):
                for j in range(2):
                    v_copy(b, b, j)
            for b, p, i, left in peeled_batches(act):
                for s in range(STEPS):
                    exps(b, s, 0)
                    if left == 2 and s - 2 in QK_STEPS:
                        part2(b + 2, QK_STEPS.index(s - 2))
                    exps(b, s, 1)
                    if left and s in LN_STEPS:
                        ln_copy(act, b + 10, p, LN_STEPS.index(s))
                    if left and s in NEG_STEPS:
                        nt_copy(b + 1, NEG_STEPS.index(s))
                    if left == 2 and s in QK_STEPS:
                        part1(b + 2, QK_STEPS.index(s), 7)
                    if s + 1 in OUT_STEPS:
                        u_copy(b, OUT_STEPS.index(s + 1))
                u_copy(b, GR - 1)
                if left == 2:
                    for j in range(2):
                        v_copy(b + 2, p, j)
                if left:
                    nt_copy(b + 1, GR - 1)
                if left == 0:
                    high_part(act, 4, 12, 0)
                act.wait_ge(ob_mm, 2 * b + 1)
                nc.scalar.activation(OT[:, 0], PS[:, 2], ACT.Copy).then_inc(o_ready, 1)
            act.wait_ge(gscale, 4)
            for b, p in batches(act):
                for j in range(DC):
                    act.wait_ge(ff_mm, DC * b + j + 1)
                    need(act, yf_part, DC * b + j - DLAG)
                    nc.scalar.activation(GE[:, j % (DLAG + 1)], PS[:, j % 4], ACT.Gelu,
                                         bias=B1[:, j:j + 1]).then_inc(ge_ready, 1)
                    need(act, ge_ready, DC * b + j + 1)
                    nc.scalar.activation(GH[:, j % (DLAG + 1)], GE[:, j % (DLAG + 1)], ACT.Copy,
                                         scale=GSC[:, 0:1]).then_inc(gh_ready, 1)
                    if j == 6:
                        for c in range(CT):
                            ln_copy(act, 13 + b, 1 - p, c, 7 - 3 * c)
                high_part(act, 5 + b, 13 + b, 1 - p)

        @block.vector
        def _(dve):
            dve.wait_ge(x_first, 16)
            ln_stats_of(dve, 0, 0, 0)
            ln_scale(dve, 0, 0, 0)
            dve.wait_ge(x_rest, 16 * (B - 1))
            for b, p in batches(dve):
                hold(dve, resid_a, 2 * b)
                ln_stats_of(dve, b + 1, 1 - p, following(b, p))
                for c in range(CT):
                    if c:
                        ln_scale(dve, b + 1, 1 - p, following(b, p))
                    need(dve, scan_act, 4 * b + 2 * c + 2)
                    nc.vector.tensor_tensor_scan(HS[:, p, c], GV[:, p, c], GV[:, p, 2 + c], 0.0,
                                                 ALU.mult, ALU.add).then_inc(scanned, 1)
                dve.wait_ge(fc_in, 16)
                nc.vector.tensor_reduce(FMAX[:, bass.ds(b, 1)], FCRAW[:, bass.ds(FC * FCW // B * b, FC * FCW // B)],
                                        AX.X, ALU.max, apply_absolute_value=True).then_inc(fmax, 1)
                for j in range(2):
                    dve.wait_ge(back_mm, 2 * b + j + 1)
                    xs = X[:, tiles(b, 2 * j, 2)]
                    nc.vector.tensor_tensor(xs, PS[:, 4 + j].rearrange("p (t c) -> p t c", t=2), xs,
                                            ALU.add).then_inc(resid_a, 1)
            V = nc.vector
            dve.wait_ge(fmax, B)
            V.tensor_reduce(FMAX[:, B:B + 1], FMAX[:, 0:B], AX.X, ALU.max).then_inc(fmax, 1)
            dve.wait_ge(fmax_t, 1)
            V.tensor_reduce(FMAXT[:], PS[0:1, 6, 0:P], AX.X, ALU.max).then_inc(fscale, 1)
            dve.wait_ge(fscale, 1)
            V.tensor_scalar(FMAXT[:], FMAXT[:], 1e-30, None, ALU.max).then_inc(fscale, 1)
            dve.wait_ge(fscale, 2)
            V.tensor_scalar(FMAXT[:].bitcast(i32), FMAXT[:].bitcast(i32), 0x7f800000, None,
                            ALU.bitwise_and).then_inc(fscale, 1)
            dve.wait_ge(fscale, 3)
            V.tensor_scalar(FSC[:, 0:1].bitcast(i32), FMAXT[:].bitcast(i32), -1.0,
                            float((254 + TOPEXP) << 23), ALU.mult, ALU.add).then_inc(fscale, 1)
            V.tensor_scalar(FSC[:, 1:2], FMAXT[:], 2.0 ** -TOPEXP, None, ALU.mult).then_inc(fscale, 1)
            dve.wait_ge(fsc_mm, 1)
            V.tensor_copy(SCALE[:], PS[:, 6, P:P + 2]).then_inc(scale_ready, 1)
            low_part(dve, 0, 0)
            dve.wait_ge(scale_ready, 1)
            for k, (j0, j1) in enumerate(zip(GROUPS, GROUPS[1:])):
                part = slice(FCW * j0, FCW * j1)
                dve.wait_ge(fch_ready, k + 1)
                if k:
                    dve.wait_ge(fcl_ready, k)
                V.scalar_tensor_tensor(FCL[:, part], FCRAW[:, part], SCALE[:, 0:1], FCH[:, part],
                                       ALU.mult, ALU.subtract).then_inc(fcl_ready, 1)
            def rest1(b, k, bank):
                dve.wait_ge(q_part1, 4 * b + k + 1)
                need(dve, q_part3, 4 * b + k - 1)
                V.tensor_tensor(rest_of(b, k), PS[:, bank], parts_of(b, QK_ORDER[k])[:, 0],
                                ALU.subtract).then_inc(q_rest, 1)

            def top(b, q, k, bank):
                dve.wait_ge(top_mm, 64 * b + k + 1)
                V.tensor_reduce(MX[:, q, k // TT, k % TT:k % TT + 1], PS[:, bank], AX.X, ALU.max
                                ).then_inc(top_ready, 1)

            def negate(b, q, g):
                need(dve, top_ready, 64 * b + 16 * g + 16)
                m = MX[:, q, HG * g:HG * (g + 1)]
                part = [NP[:, g % 2, :, n].rearrange("p t h -> p h t") for n in range(3)]
                k0 = 16 * b + 4 * g
                V.tensor_scalar(part[0], m, -1.0, None, ALU.mult).then_inc(neg_step, 1)
                dve.wait_ge(neg_step, k0 + 1)
                V.scalar_tensor_tensor(NREM[:], m, -1.0, part[0], ALU.mult, ALU.subtract).then_inc(neg_step, 1)
                dve.wait_ge(neg_step, k0 + 2)
                V.tensor_copy(part[1], NREM[:]).then_inc(neg_step, 1)
                dve.wait_ge(neg_step, k0 + 3)
                V.tensor_tensor(part[2], NREM[:], part[1], ALU.subtract).then_inc(neg_step, 1)

            def add_c(b):
                for j in range(2):
                    dve.wait_ge(wo_mm, 2 * b + j + 1)
                    xs = X[:, tiles(b, 2 * j, 2)]
                    V.tensor_tensor(xs, PS[:, 6 + j].rearrange("p (t c) -> p t c", t=2), xs, ALU.add
                                    ).then_inc(resid_c, 1)

            def normalise(b, g):
                dve.wait_ge(ut_mm, 4 * b + g + 1)
                ut = MISC.rearrange("p (t h d) -> p t h d", t=TT, h=HG)
                V.reciprocal(RECIP[:, g % 2], ut[:, :, :, HD]).then_inc(recip_ready, 1)
                dve.wait_ge(recip_ready, 4 * b + g + 1)
                V.tensor_tensor(OTOK[:, :, HG * g:HG * (g + 1)], ut[:, :, :, 0:HD],
                                RECIP[:, g % 2].unsqueeze(3).broadcast_to([P, TT, HG, HD]),
                                ALU.mult).then_inc(otok_ready, 1)

            RS = 13

            def router(b, k0, ops):
                for k, op in enumerate(ops, k0):
                    if k:
                        dve.wait_ge(router_step, RS * b + k)
                    op().then_inc(router_step, 1)

            def bc_i(a):
                return a.unsqueeze(2).broadcast_to([P, TT, NE, NE])

            def bc_j(a):
                return a.unsqueeze(3).broadcast_to([P, TT, NE, NE])

            def bc_e(a, n=NE):
                return a.unsqueeze(2).broadcast_to([P, TT, n])

            LG = MISC[:, 0:16 * TT].rearrange("p (t e) -> p t e", t=TT)
            for b, p, i, left in peeled_batches(dve):
                hold(dve, resid_b, 2 * b)
                for j in range(FC + LAG):
                    tops = tops_at(j) if left == 0 else []
                    early = 1 if tops and tops[0][1] == 4 else 2
                    if left == 1 and j in QK0_AT:
                        rest1(0, QK0_AT.index(j), 7)
                    for k, bank in tops[:early]:
                        top(0, 0, k, bank)
                    if j < FC:
                        wd = width(j)
                        need(dve, silu_ready, FC * b + j + 1)
                        dve.wait_ge(h2_mm, FC * b + j + 1)
                        V.scalar_tensor_tensor(UP[0:wd, j % (LAG + 2)], PS[0:wd, 2 + j % 2], SCALE[0:wd, 1:2],
                                               SILU[0:wd, j % 2], ALU.mult, ALU.mult).then_inc(up_ready, 1)
                    if j == 0:
                        dve.wait_ge(logit_t, b + 1)
                        router(b, 0, [lambda: V.tensor_reduce(ROWMAX[:], LG[:, :, 0:NE], AX.X, ALU.max)])
                        dve.wait_ge(router_step, RS * b + 1)
                        V.tensor_tensor(ZE[:], LG[:, :, 0:NE], bc_e(ROWMAX[:]), ALU.subtract).then_inc(router_z, 1)
                        V.tensor_copy(ZS[:], LG[:, :, NE]).then_inc(router_z, 1)
                    for k, bank in tops[early:early + 1]:
                        top(0, 0, k, bank)
                    if left and j == 11:
                        low_part(dve, b + 1, 1 - p)
                    if j == 1:
                        dve.wait_ge(router_e, 2 * b + 2)
                        router(b, 1, [
                            lambda: V.tensor_reduce(ESUM[:], EE[:], AX.X, ALU.add),
                            lambda: V.reciprocal(ERCP[:], ESUM[:]),
                            lambda: V.tensor_tensor(GT[:], bc_i(EE[:]), bc_j(EE[:]), ALU.is_gt),
                            lambda: V.tensor_tensor(EQ[:], bc_i(EE[:]), bc_j(EE[:]), ALU.is_equal),
                            lambda: V.tensor_tensor(EQ[:], EQ[:], LOWER[:].unsqueeze(1).broadcast_to(
                                [P, TT, NE, NE]), ALU.mult),
                            lambda: V.tensor_tensor(GT[:], GT[:], EQ[:], ALU.add),
                        ])
                    if j == 2:
                        router(b, 7, [
                            lambda: V.tensor_reduce(RANK[:], GT[:], AX.X, ALU.add),
                            lambda: V.scalar_tensor_tensor(SELE[:], RANK[:], TOPK - 0.5, EE[:],
                                                           ALU.is_lt, ALU.mult),
                            lambda: V.tensor_tensor(COMB[:, :, 0:NE], SELE[:], bc_e(ERCP[:]), ALU.mult),
                            lambda: V.tensor_scalar(ESUM[:], ES[:], 1.0, None, ALU.add),
                            lambda: V.reciprocal(COMB[:, :, NE], ESUM[:]),
                            lambda: V.tensor_copy(CPART[:, :, 0], COMB[:]),
                        ])
                        assert RS == 13
                        dve.wait_ge(router_step, RS * b + RS)
                        V.tensor_tensor(CREM[:], COMB[:], CPART[:, :, 0], ALU.subtract).then_inc(comb_step, 1)
                        dve.wait_ge(comb_step, 3 * b + 1)
                        V.tensor_copy(CPART[:, :, 1], CREM[:]).then_inc(comb_step, 1)
                        dve.wait_ge(comb_step, 3 * b + 2)
                        V.tensor_tensor(CPART[:, :, 2], CREM[:], CPART[:, :, 1], ALU.subtract).then_inc(comb_step, 1)
                    n, q, src = (5 + b, 1 - p, b + 1) if left else (9, 1, 1)
                    if j == 4:
                        ln_stats_of(dve, n, q, src)
                    if j == 6:
                        ln_scale(dve, n, q, src)
                    if left == 1 and j == 5:
                        ln_stats_of(dve, 8, 0, 0)
                    if left == 1 and j == 9:
                        ln_scale(dve, 8, 0, 0)
                    jw = j - LAG
                    if jw >= 0:
                        wd = width(jw)
                        dve.wait_ge(c_mm, FC * b + jw + 1)
                        need(dve, up_ready, FC * b + jw + 1)
                        need(dve, y_part, FC * b + jw - 2)
                        V.tensor_tensor(HID[0:wd, jw % 3], PS[0:wd, 4], UP[0:wd, jw % (LAG + 2)],
                                        ALU.mult).then_inc(hid_ready, 1)
                    for k, bank in tops[early + 1:]:
                        top(0, 0, k, bank)
                    if left == 0 and j + 1 in NEG0_AT:
                        negate(0, 0, NEG0_AT.index(j + 1))
                    if left == 0 and j in QK1_AT:
                        rest1(1, QK1_AT.index(j), QK1_AT.index(j))
                need(dve, y_part, FC * b + FC)
                for j in range(2):
                    xs = X[:, tiles(b, 2 * j, 2)]
                    V.tensor_tensor(xs, y_bank(j), xs, ALU.add).then_inc(resid_b, 1)

            def dense_scale():
                dve.wait_ge(gmax, 1)
                V.tensor_scalar(GMAX[:, 1:2], GMAX[:, 0:1], float(XNORM2), None, ALU.add).then_inc(gscale, 1)
                dve.wait_ge(gscale, 1)
                V.tensor_scalar(GMAX[:, 0:1].bitcast(i32), GMAX[:, 1:2].bitcast(i32), 0x7f800000, None,
                                ALU.bitwise_and).then_inc(gscale, 1)
                dve.wait_ge(gscale, 2)
                V.tensor_scalar(GSC[:, 0:1].bitcast(i32), GMAX[:, 0:1].bitcast(i32), -1.0,
                                float((254 + GEXP) << 23), ALU.mult, ALU.add).then_inc(gscale, 1)
                V.tensor_scalar(GSC[:, 1:2], GMAX[:, 0:1], 2.0 ** -GEXP, None, ALU.mult).then_inc(gscale, 1)
                dve.wait_ge(gscale, 4)

            need(dve, resid_b, 2 * B)
            ln_stats_of(dve, 10, 0, 2)
            dve.wait_ge(ffn_in, 64)
            V.tensor_reduce(BMAX[:], B1[:], AX.X, ALU.max, apply_absolute_value=True).then_inc(gbound, 1)
            for b, p, i, left in peeled_batches(dve):
                if left == 0:
                    dense_scale()
                src = b + 2 if left == 2 else 0
                for s in range(STEPS):
                    if left and s == 1:
                        hold(dve, ln_rstd, b + 11)
                    for k in range(4):
                        if left:
                            top(b + 1, 1 - p, 4 * s + k, k % 2)
                            if s == 1:
                                ln_scale_tile(p, src, k)
                        if left == 2 and k == 1 and s - 1 in QK_STEPS:
                            rest1(b + 2, QK_STEPS.index(s - 1), 7)
                        if k == 1 and s - 1 in OUT_STEPS:
                            normalise(b, OUT_STEPS.index(s - 1))
                    if left and s % 4 == 3:
                        negate(b + 1, 1 - p, s // 4)
                normalise(b, GR - 1)
                dve.wait_ge(ob_mm, 2 * b + 2)
                V.tensor_copy(OT[:, 1], PS[:, 3]).then_inc(o_ready, 1)
                if left == 0:
                    low_part(dve, 4, 0)
                if left == 2:
                    ln_stats_of(dve, b + 11, 1 - p, b + 3 if p == 0 else b - 1)
                add_c(b)

            for b, p in batches(dve):
                hold(dve, resid_d, 2 * b)
                for j in range(DC):
                    need(dve, ge_ready, DC * b + j + 1)
                    need(dve, yf_part, DC * b + j - DLAG)
                    dve.wait_ge(gh_ready, DC * b + j + 1)
                    V.scalar_tensor_tensor(GL[:, j % (DLAG + 1)], GE[:, j % (DLAG + 1)], GSC[:, 0:1],
                                           GH[:, j % (DLAG + 1)], ALU.mult, ALU.subtract).then_inc(gl_ready, 1)
                    if j in (3, 4):
                        if j == 3:
                            hold(dve, xn_ready, TT * (12 + b) + TT)
                        xs = X[:, tiles(b, 2 * (j - 3), 2)]
                        V.tensor_tensor(xs, xs, B2[:].unsqueeze(1).broadcast_to([P, 2, C]), ALU.add
                                        ).then_inc(b2_added, 1)
                    if j == 0:
                        ln_stats_of(dve, 13 + b, 1 - p, following(b, p))
                    if j == 2:
                        ln_scale(dve, 13 + b, 1 - p, following(b, p))
                low_part(dve, 5 + b, 1 - p)
                need(dve, yf_part, DC * b + DC)
                dve.wait_ge(b2_added, 2 * b + 2)
                for j in range(2):
                    xs = X[:, tiles(b, 2 * j, 2)]
                    V.scalar_tensor_tensor(xs, y_bank(j), GSC[:, 1:2], xs, ALU.mult, ALU.add).then_inc(resid_d, 1)

        @block.tensor
        def _(pe):
            MM = nc.tensor.matmul
            pe.wait_ge(ident_in, 16)
            for c in range(CT):
                ln_transpose(pe, 0, 0, c, 7 - c)
            pe.wait_ge(w0_in, 32)
            for b, p in batches(pe):
                pe.wait_ge(xnt_ready, 2 * b + 2)
                for k, m in enumerate((0, 2, 1, 3)):
                    need(pe, scan_act, 4 * b + k - 3)
                    for c in range(CT):
                        mm = MM(PS[:, m], W0[:, c, m * P:(m + 1) * P], XNT[:, p, c], start=c == 0, stop=c == CT - 1)
                    mm.then_inc(scan_mm, 1)
                for c in range(CT):
                    ln_transpose(pe, b + 1, 1 - p, c, 7 - c)
                pe.wait_ge(scanned, 2 * b + 2)
                need(pe, resid_a, 2 * b)
                for t in range(TT):
                    for c in range(CT):
                        mm = nc.tensor.transpose(PS[:, 4 + t // 2, (t % 2) * C + c * P:(t % 2) * C + (c + 1) * P],
                                                 HS[:, p, c, t * P:(t + 1) * P], IDENT[:])
                    if t % 2:
                        mm.then_inc(back_mm, 1)
            pe.wait_ge(ones_set, 1)
            pe.wait_ge(xnt_ready, 10)
            pe.wait_ge(fmax, B + 1)
            nc.tensor.transpose(PS[0:1, 6, 0:P], FMAX[:, B:B + 1], IDENT[:]).then_inc(fmax_t, 1)
            pe.wait_ge(fscale, 5)
            MM(PS[:, 6, P:P + 2], ONES[0:1], FSC[:], start=True, stop=True).then_inc(fsc_mm, 1)
            pe.wait_ge(mix_in, 32)
            pe.wait_ge(attn_in, 64)
            pe.wait_ge(const_in, 48)
            def qk_project(b, q, k, bank):
                w = QK_ORDER[k]
                for c in range(CT):
                    mm = MM(PS[:, bank], (WQ, WK)[w // 2][:, c, (w % 2) * P:(w % 2 + 1) * P], XNT[:, q, c],
                            start=c == 0, stop=c == CT - 1)
                mm.then_inc(q_mm, 1)

            def v_project(q, t):
                for c in range(CT):
                    mm = MM(PS[:, t // 2, (t % 2) * C:(t % 2 + 1) * C], XNT[:, q, c, t * P:(t + 1) * P],
                            WV[:, c], start=c == 0, stop=c == CT - 1)
                if t % 2:
                    mm.then_inc(v_mm, 1)

            def top_scores(b, q, k, bank):
                h, t = divmod(k, TT)
                if bank < 2:
                    need(pe, top_ready, 64 * b + k - 1)
                MM(PS[:, bank], QS[q][0:KROWS, h, t * P:(t + 1) * P], KS[q][0:KROWS, h],
                   start=True, stop=True).then_inc(top_mm, 1)

            def neg_transpose(b, g):
                pe.wait_ge(neg_step, 16 * b + 4 * g + 4)
                for t in range(TT):
                    mm = nc.tensor.transpose(MISCB[0:3 * HG, t * P:(t + 1) * P],
                                             NP[:, g % 2, t].rearrange("p n h -> p (n h)"), IDENTB[:])
                mm.then_inc(neg_t, 1)

            def scores(b, q, s, j):
                g, kt = divmod(s, TT)
                need(pe, exp_done, 32 * b + 2 * s + j - 1)
                for k in range(2):
                    mm = MM(PS[:, 2 + 2 * j + k], KS[q][0:MROWS, HG * g + 2 * j + k, kt * P:(kt + 1) * P],
                            QS[q][0:MROWS, HG * g + 2 * j + k], start=True, stop=True)
                mm.then_inc(s_mm, 1)

            def weigh(b, q, s):
                g, kt = divmod(s, TT)
                need(pe, exp_done, 32 * b + 2 * s + 2)
                if kt == 0:
                    need(pe, u_ready, 4 * b + g)
                for k in range(HG):
                    mm = MM(PS[32 * k:32 * k + 32, 6], VA[:, q, kt, HG * g + k], PR[:, kt % 2, k],
                            start=kt == 0, stop=kt == TT - 1)
                mm.then_inc(pv_done, 1)

            def turn_output(b, g):
                need(pe, u_ready, 4 * b + g + 1)
                for t in range(TT):
                    mm = nc.tensor.transpose(MISC[:, t * P:(t + 1) * P], U[:, g % 2, t * P:(t + 1) * P], IDENT[:])
                mm.then_inc(ut_mm, 1)

            def turn_back(c):
                for t in range(TT):
                    mm = nc.tensor.transpose(PS[:, 2 + c, t * P:(t + 1) * P],
                                             OTOK[:, t, c * H // 2:(c + 1) * H // 2].rearrange("p h d -> p (h d)"),
                                             IDENT[:])
                mm.then_inc(ob_mm, 1)

            def out_project(b, j):
                for t in (2 * j, 2 * j + 1):
                    for c in range(CT):
                        mm = MM(PS[:, 6 + j, (t % 2) * C:(t % 2 + 1) * C], OT[:, c, t * P:(t + 1) * P],
                                WO[:, c], start=c == 0, stop=c == CT - 1)
                mm.then_inc(wo_mm, 1)

            def up(bank, j, f, q):
                wd = width(j)
                for c in range(CT):
                    w = slice(FCW * j + P * (CT * f + c), FCW * j + P * (CT * f + c) + wd)
                    for n, (weight, tokens) in enumerate(((FCH, XH), (FCH, XL), (FCL, XH))):
                        mm = MM(PS[0:wd, bank], weight[:, w], tokens[:, q, c],
                                start=c + n == 0, stop=c == CT - 1 and n == 2)
                return mm

            for b, p, i, left in peeled_batches(pe):
                if left == 0:
                    need(pe, q_rest, 4)
                pe.wait_ge(xnt_ready, 2 * b + 10)
                for c in range(CT):
                    mm = MM(MISC[0:NG], GATE[:, c], XNT[:, p, c], start=c == 0, stop=c == CT - 1)
                mm.then_inc(logit_mm, 1)
                free = None
                for j in range(FC + LAG + 1):
                    if j == LAG:
                        pe.wait_ge(comb_step, 3 * b + 3)
                        for t in range(TT):
                            mm = nc.tensor.transpose(MISCB[0:3 * NG, t * P:(t + 1) * P],
                                                     CPART[:, t].rearrange("p n e -> p (n e)"), IDENTB[:])
                        mm.then_inc(comb_mm, 1)
                        free = (comb_ready, b + 1)
                    if left and j in ln_at(left):
                        n, c = 5 + b, ln_at(left).index(j)
                        need(pe, *free)
                        ln_transpose(pe, n, 1 - p, c)
                        free = (xnt_ready, 2 * n + c + 1)
                    if left == 1 and j in LN8_AT:
                        c = LN8_AT.index(j)
                        need(pe, *free)
                        ln_transpose(pe, 8, 0, c)
                        free = (xnt_ready, 2 * 8 + c + 1)
                    if left == 1 and j in QK0_AT:
                        k = QK0_AT.index(j)
                        need(pe, *free)
                        qk_project(0, 0, k, 7)
                        free = (q_rest, k + 1)
                    tops = tops_at(j) if left == 0 else []

                    def maximum(free, bank=7):
                        if tops and tops[0][1] == bank:
                            k = tops.pop(0)[0]
                            need(pe, *free)
                            if k % 32 == 0:
                                pe.wait_ge(stack_in[0][k // 32], 16 * 12)
                            top_scores(0, 0, k, bank)
                            free = (top_ready, k + 1)
                        return free

                    if j < FC:
                        if j == 0:
                            pe.wait_ge(xl_ready, b + 1)
                        if j in GROUPS:
                            pe.wait_ge(fcl_ready, GROUPS.index(j) + 1)
                        need(pe, silu_ready, FC * b + j - 1)
                        up(j % 2, j, 0, p).then_inc(h1_mm, 1)
                    if left == 0 and j in ln_at(0):
                        c = ln_at(0).index(j)
                        need(pe, *free)
                        ln_transpose(pe, 9, 1, c)
                        free = (xnt_ready, 2 * 9 + c + 1)
                    elif left == 0 and j in NEG0_AT:
                        need(pe, *free)
                        neg_transpose(0, NEG0_AT.index(j))
                        free = (nt_ready, NEG0_AT.index(j) + 1)
                    else:
                        free = maximum(free)
                    free4 = maximum((hid_ready, FC * b + j - LAG), 4)
                    if j < FC:
                        need(pe, up_ready, FC * b + j - 1)
                        up(2 + j % 2, j, 1, p).then_inc(h2_mm, 1)
                    if j == 0:
                        hold(pe, logit_sb, b + 1)
                        for t in range(TT):
                            mm = nc.tensor.transpose(MISC[:, 16 * t:16 * t + NG], LOGIT[:, t * P:(t + 1) * P],
                                                     IDENT[0:NG, 0:NG])
                        mm.then_inc(logit_t, 1)
                    free = maximum(free)
                    jc = j - LAG
                    if 0 <= jc < FC:
                        if jc == 0:
                            pe.wait_ge(comb_ready, b + 1)
                            need(pe, resid_a, 2 * B)
                        need(pe, *free4)
                        MM(PS[0:width(jc), 4], SEL[:, jc * P:jc * P + width(jc)], COMBT[:, p],
                           start=True, stop=True).then_inc(c_mm, 1)
                    jp = jc - 1
                    if jp >= 0:
                        wd = width(jp)
                        if jp == 0:
                            need(pe, resid_b, 2 * b)
                        need(pe, hid_ready, FC * b + jp + 1)
                    for t in range(TT):
                        if jp >= 0:
                            mm = MM(y_bank(t // 2)[:, t % 2], HID[0:wd, jp % 3, t * P:(t + 1) * P],
                                    PROJ[0:wd, jp], start=jp == 0 and t % 2 == 0, stop=jp == FC - 1,
                                    skip_group_check=True)
                        if t % 2:
                            free = maximum(free)
                    if jp >= 0:
                        mm.then_inc(y_part, 1)
                    if left == 0 and j in QK1_AT:
                        k = QK1_AT.index(j)
                        need(pe, (silu_ready, up_ready)[k // 2], FC * B)
                        qk_project(1, 1, k, k)

            need(pe, q_rest, 8)
            for b in range(2):
                for t in range(TT):
                    if t % 2 == 0:
                        need(pe, v_ready, 2 * b + t // 2 - 1)
                    v_project(b, t)
            need(pe, resid_b, 2 * B)
            pe.wait_ge(nt_ready, GR)
            pe.wait_ge(k_ones, 32)
            for b, p, i, left in peeled_batches(pe):
                free = (resid_c, 2 * b)
                if left:
                    need(pe, v_ready, 2 * b + 4)
                for s in range(STEPS):
                    g, kt = divmod(s, TT)
                    if left:
                        if s % 8 == 0:
                            pe.wait_ge(stack_in[1 - p][s // 8], 16 * 12 * (i + p + 1))
                        top_scores(b + 1, 1 - p, 4 * s, 0)
                    if kt == 0:
                        pe.wait_ge(nm_in[g], 16 * b + 16)
                    scores(b, p, s, 0)
                    if left:
                        top_scores(b + 1, 1 - p, 4 * s + 1, 1)
                    scores(b, p, s, 1)
                    if left:
                        top_scores(b + 1, 1 - p, 4 * s + 2, 0)
                    if s == 1:
                        need(pe, resid_c, 2 * b)
                    if s:
                        weigh(b, p, s - 1)
                    if left:
                        top_scores(b + 1, 1 - p, 4 * s + 3, 1)
                    if left and s in LN_STEPS:
                        c = LN_STEPS.index(s)
                        need(pe, *free)
                        ln_transpose(pe, b + 10, p, c)
                        free = (xnt_ready, 2 * b + 20 + c + 1)
                    if s in OUT_STEPS:
                        need(pe, *free)
                        turn_output(b, g - 1)
                        free = (otok_ready, 4 * b + g)
                    if left and s in NEG_STEPS:
                        need(pe, *free)
                        neg_transpose(b + 1, g - 1)
                        free = (nt_ready, 4 * b + 4 + g)
                    if left == 2 and s in QK_STEPS:
                        k = QK_STEPS.index(s)
                        need(pe, *free)
                        if k == 0:
                            pe.wait_ge(xnt_ready, 2 * b + 22)
                        qk_project(b + 2, p, k, 7)
                        free = (q_rest, 4 * b + 8 + k + 1)
                weigh(b, p, STEPS - 1)
                if left:
                    need(pe, top_ready, 64 * b + 128)
                if left == 2:
                    v_project(p, 0)
                need(pe, *free)
                turn_output(b, GR - 1)
                if left == 2:
                    v_project(p, 1)
                pe.wait_ge(otok_ready, 4 * b + GR)
                for c in range(CT):
                    turn_back(c)
                if left == 2:
                    v_project(p, 2)
                    v_project(p, 3)
                if left:
                    neg_transpose(b + 1, GR - 1)
                pe.wait_ge(o_ready, 2 * b + 2)
                out_project(b, 0)
                if left:
                    pe.wait_ge(nt_ready, 4 * b + 4 + GR)
                out_project(b, 1)

            pe.wait_ge(tern_ready, 4)
            for b, p in batches(pe):
                pe.wait_ge(xl_ready, b + 5)
                for j in range(DC + DLAG):
                    if j < DC:
                        need(pe, ge_ready, DC * b + j - 3)
                        for c in range(CT):
                            for n, tokens in enumerate((XH, XL)):
                                mm = MM(PS[:, j % 4], W1Q[:, c, j * P:(j + 1) * P], tokens[:, p, c],
                                        start=c + n == 0, stop=c == CT - 1 and n == 1)
                        mm.then_inc(ff_mm, 1)
                    if j == 6:
                        for c in range(CT):
                            ln_transpose(pe, 13 + b, 1 - p, c, 7 - 3 * c)
                    jp = j - DLAG
                    if jp >= 0:
                        if jp == 0:
                            need(pe, resid_d, 2 * b)
                            need(pe, resid_c, 2 * B)
                        pe.wait_ge(gl_ready, DC * b + jp + 1)
                        for t in range(TT):
                            for n, hidden in enumerate((GH, GL)):
                                mm = MM(y_bank(t // 2)[:, t % 2], hidden[:, jp % (DLAG + 1), t * P:(t + 1) * P],
                                        W2Q[:, jp], start=jp + n == 0 and t % 2 == 0, stop=jp == DC - 1 and n == 1,
                                        skip_group_check=True)
                        mm.then_inc(yf_part, 1)


_OUT = (B, T, C)


def kernel(L0_attn_x, L0_attn_W, L0_attn_b, L0_ffn_gate_w, L0_ffn_expert_fc1, L0_ffn_expert_fc2,
           L0_ffn_expert_proj, L0_ffn_shared_fc1, L0_ffn_shared_fc2, L0_ffn_shared_proj,
           L0_ffn_shared_gate_w, L1_attn_Wq, L1_attn_Wk, L1_attn_Wv, L1_attn_Wo, L1_ffn_w1, L1_ffn_b1,
           L1_ffn_w2, L1_ffn_b2):
    import ml_dtypes
    import numpy as np
    import concourse.bacc as bacc
    from concourse.bass_utils import run_bass_kernel_spmd

    def a(v):
        return np.asarray(v)

    def rows(w):
        wt = a(w).T
        return np.ascontiguousarray(wt.reshape(-1, P, wt.shape[1]).transpose(1, 0, 2))

    fc = np.zeros((2, FC * P, C), np.float32)
    fc[0, :F] = np.concatenate([a(L0_ffn_expert_fc1).reshape(NE * FE, C), a(L0_ffn_shared_fc1)])
    fc[1, :F] = np.concatenate([a(L0_ffn_expert_fc2).reshape(NE * FE, C), a(L0_ffn_shared_fc2)])
    fc = fc.reshape(2, FC, P, CT, P).transpose(4, 1, 0, 3, 2).reshape(P, FC * FCW)
    pj = np.concatenate([a(L0_ffn_expert_proj).transpose(0, 2, 1).reshape(NE * FE, C),
                         a(L0_ffn_shared_proj).T])
    pj = np.concatenate([pj, np.zeros((FC * P - F, C), pj.dtype)])
    expert_of = np.minimum(np.arange(F) // FE, NE)
    low = np.arange(NE)[None, :] < np.arange(NE)[:, None]
    data = {
        "x": a(L0_attn_x),
        "w0": rows(L0_attn_W),
        "b0": np.ascontiguousarray(a(L0_attn_b).reshape(4, P).T),
        "fc": np.ascontiguousarray(fc),
        "proj": np.ascontiguousarray(pj.reshape(FC, P, C).transpose(1, 0, 2)),
        "gate": rows(np.concatenate([a(L0_ffn_gate_w), a(L0_ffn_shared_gate_w)])),
        "sel": np.tile(np.arange(NG)[:, None] == expert_of[None, :], (3, 1)).astype(ml_dtypes.bfloat16),
        "wq": rows(L1_attn_Wq), "wk": rows(L1_attn_Wk), "wv": rows(L1_attn_Wv),
        "wo": rows(L1_attn_Wo),
        "w1": rows(L1_ffn_w1),
        "b1": np.ascontiguousarray(a(L1_ffn_b1).reshape(DC, P).T),
        "w2": rows(L1_ffn_w2),
        "b2": np.ascontiguousarray(np.broadcast_to(a(L1_ffn_b2), (P, C))),
        "ident": np.eye(P, dtype=np.float32),
        "identb": np.eye(P, dtype=np.float32).astype(ml_dtypes.bfloat16),
        "kones": np.ones((MROWS - KROWS, H, T), ml_dtypes.bfloat16),
        "lower": np.ascontiguousarray(np.broadcast_to(low, (P, NE, NE))).astype(np.float32),
    }
    nc = bacc.Bacc("TRN2", target_bir_lowering=False, num_devices=1)
    arrays, args = {}, {}
    for name, v in data.items():
        arrays[f"in_{name}"] = v
        args[name] = nc.dram_tensor(f"in_{name}", v.shape, mybir.dt.from_np(v.dtype), kind="ExternalInput").ap()
    args["out"] = nc.dram_tensor("out_0", _OUT, mybir.dt.float32, kind="ExternalOutput").ap()
    build(nc, **args)
    r = run_bass_kernel_spmd(nc, [arrays], core_ids=[0])
    return r.results[0]["out_0"]
```
